# Optimizing a Trainium2 kernel written in Bass

```python
import numpy as np
import jax
import jax.numpy as jnp

def _softmax(x, axis=-1):
    return jax.nn.softmax(x, axis=axis)

def _gelu(x):
    return jax.nn.gelu(x, approximate=True)

def _silu(x):
    return jax.nn.silu(x)

def _sigmoid(x):
    return jax.nn.sigmoid(x)

def _layernorm(x, axis=-1, eps=1e-05):
    m = jnp.mean(x, axis=axis, keepdims=True)
    v = jnp.var(x, axis=axis, keepdims=True)
    return (x - m) / jnp.sqrt(v + eps)

def _scatter_add(tgt, idx, src, axis=0):
    return tgt.at[idx].add(src)

def _segment_sum(src, seg, n):
    return jax.ops.segment_sum(src, seg, n)
kernel_name = 'mk_gnn_preln_d1_gnn_r32_8086b9'

def setup_inputs(seed: int=0):
    np.random.seed(seed)
    _w = jnp.asarray

    def _rec_inputs():
        import jax
        import jax.numpy as jnp
        _gk = jax.random.key(seed)
        x = -0.000202 + 1 * jax.random.normal(jax.random.fold_in(_gk, 1), (50000, 128), jnp.float32)
        src = jax.random.randint(jax.random.fold_in(_gk, 2), (50000,), 0, 50000, jnp.int32)
        dst = jax.random.randint(jax.random.fold_in(_gk, 3), (50000,), 0, 50000, jnp.int32)
        _o = jnp.argsort(dst, stable=True)
        src = src[_o]
        dst = dst[_o]
        edge_attr_64 = 0.000155561 + 1.00019 * jax.random.normal(jax.random.fold_in(_gk, 11), (50000, 64), jnp.float32)
        return (x, src, dst, edge_attr_64)
    x, src, dst, edge_attr_64 = _rec_inputs()

    def _L0_gnn_setup():
        import jax, jax.numpy as jnp
        import numpy as np
        N_NODES, N_EDGES = (50000, 18750)
        NODE_DIM, EDGE_DIM = (128, 64)
        H, HD = (4, 32)
        key = jax.random.key(seed)
        k = jax.random.split(key, 6)
        node_features = jax.random.normal(k[0], (N_NODES, NODE_DIM), jnp.float32)
        edge_indices = jax.random.randint(k[1], (2, N_EDGES), 0, N_NODES, jnp.int32)
        edge_features = jax.random.normal(k[2], (N_EDGES, EDGE_DIM), jnp.float32)
        W_node = jax.random.normal(k[3], (H * HD, NODE_DIM), jnp.float32) / np.sqrt(NODE_DIM).astype(np.float32)
        W_edge = jax.random.normal(k[4], (H * HD, EDGE_DIM), jnp.float32) / np.sqrt(EDGE_DIM).astype(np.float32)
        a = jax.random.normal(k[5], (H, 3 * HD), jnp.float32)
        return {'node_features': node_features, 'edge_indices': edge_indices, 'edge_features': edge_features, 'W_node': W_node, 'W_edge': W_edge, 'a': a}
    _L0_gnn_all = _L0_gnn_setup()
    _L0_gnn_in = {k: v for k, v in _L0_gnn_all.items() if k in ('W_node', 'W_edge', 'a')}
    del _L0_gnn_all
    return {'x': x, 'src': src, 'dst': dst, 'edge_attr_64': edge_attr_64, 'L0_gnn_W_node': _L0_gnn_in['W_node'], 'L0_gnn_W_edge': _L0_gnn_in['W_edge'], 'L0_gnn_a': _L0_gnn_in['a']}

def reference(x, src, dst, edge_attr_64, L0_gnn_W_node, L0_gnn_W_edge, L0_gnn_a):
    import jax
    import jax.numpy as jnp

    def _L0_gnn_ref(node_features, edge_indices, edge_features, W_node, W_edge, a):
        import jax, jax.numpy as jnp
        import numpy as np
        N_NODES, N_EDGES = (50000, 18750)
        NODE_DIM, EDGE_DIM = (128, 64)
        H, HD = (4, 32)
        num_nodes = node_features.shape[0]
        num_edges = edge_indices.shape[1]
        h = (node_features @ W_node.T).reshape(num_nodes, H, HD)
        e = (edge_features @ W_edge.T).reshape(num_edges, H, HD)
        src, tgt = (edge_indices[0], edge_indices[1])
        h_src = h[src]
        h_tgt = h[tgt]
        att_in = jnp.concatenate([h_src, h_tgt, e], axis=-1)
        att = jnp.sum(att_in * a, axis=-1)
        att = jnp.where(att > 0, att, 0.2 * att)
        m = jnp.maximum(jax.ops.segment_max(att, tgt, num_segments=num_nodes), 0.0)
        ex = jnp.exp(att - m[tgt])
        ones = jnp.ones((num_edges,), node_features.dtype)
        deg = jax.ops.segment_sum(ones, tgt, num_segments=num_nodes)
        denom = jax.ops.segment_sum(ex, tgt, num_segments=num_nodes) + (num_edges - deg)[:, None] * jnp.exp(-m)
        w = ex / denom[tgt]
        h_prime = jax.ops.segment_sum(w[:, :, None] * h_src, tgt, num_segments=num_nodes)
        return h_prime.reshape(num_nodes, H * HD)
    edge_index = jnp.stack([src, dst])
    h = jnp.maximum(_layernorm(x, axis=-1), 0.0)
    x = x + _L0_gnn_ref(h, edge_index, edge_attr_64, L0_gnn_W_node, L0_gnn_W_edge, L0_gnn_a)
    return x

_drawn_inputs = setup_inputs


def setup_inputs(seed=0):
    import zlib

    import numpy as np

    out = dict(_drawn_inputs(seed))
    spreads = {}
    factors = {}
    for name, (base, spread) in spreads.items():
        noise = np.random.default_rng([zlib.crc32(name.encode()), seed]).standard_normal(out[name].shape)
        drawn = base * np.exp(spread * noise) if base else spread * noise
        out[name] = jnp.asarray(drawn.astype(out[name].dtype))
    for name, factor in factors.items():
        out[name] = (out[name] * factor).astype(out[name].dtype)
    return out
```

```python
import itertools

import numpy as np

import concourse.bass as bass
from concourse import mybir
from contextlib import ExitStack


LOOP = 20


class Step:

    def __init__(self, turn, at):
        self.turn, self.at = turn, at

    def __add__(self, n):
        return Step(self.turn, self.at + n)

    def value(self, scale=1, plus=0):
        const = scale * self.at + plus
        return const if self.turn is None else self.turn * (LOOP * scale) + const

    def turns(self, ring, scale=1, plus=0):
        const = scale * (self.at // ring) + plus
        return const if self.turn is None else self.turn * (LOOP // ring * scale) + const


def general_path(nc, x, src, dst, edge, out, flag, w_h, w_tgt, w_edge, ident, ones, ring, banks):
    f32, i32 = mybir.dt.float32, mybir.dt.int32
    ALU, ACT, AX = mybir.AluOpType, mybir.ActivationFunctionType, mybir.AxisListType

    N, D = x.shape
    E, K = edge.shape
    H = w_tgt.shape[1]
    HD = D // H
    HC = D + H
    EPS = 1e-5
    NEWTON = 3
    GT = 125
    TILES = E // GT
    assert TILES * GT == E and N == E

    node_table = nc.dram_tensor("node_table_scratch", (N, HC + H), f32, kind="Internal").ap()
    max_table = nc.dram_tensor("max_table_scratch", (N, H), f32, kind="Internal").ap()
    sum_table = nc.dram_tensor("sum_table_scratch", (N, H + 1), f32, kind="Internal").ap()
    edge_scratch = nc.dram_tensor("edge_scratch", (E, K), f32, kind="Internal").ap()

    ctx = ExitStack()
    with ctx:
        used = 0

        def tile(width):
            nonlocal used
            used += width
            return ring[0:GT, used - width:used]

        def sem(name):
            return ctx.enter_context(nc.semaphore(name))

        rows, centred, squares, relu, relu_T = tile(D), tile(D), tile(D), tile(D), ring[0:D, 4 * D:4 * D + GT]
        used += D
        total, mean, square_sum, variance, rstd, root = (tile(1) for _ in range(6))
        node_row, zeros = tile(HC + H), tile(H + 1)
        src_id, dst_id, dst_ids = tile(1).bitcast(i32), tile(1).bitcast(i32), tile(GT).bitcast(i32)
        dst_f, dst_fs, equal = tile(1), tile(GT), tile(GT)
        feat, feat_T = tile(2 * K), ring[:, used:used + GT]
        used += GT
        src_row, dst_row = tile(HC + H), tile(HC + H)
        z_a, z_b, att, positive, tile_max, old_max, new_max = (tile(H) for _ in range(7))
        spread, among = tile(H * GT), tile(H * GT)
        diff, ex, em, old_sum, new_sum = tile(H), tile(H + 1), tile(H), tile(H + 1), tile(H + 1)
        dst_max, less, rest, den, inverse, weight = tile(H), tile(1), tile(H), tile(H), tile(H), tile(H)
        message, old_out, new_out = tile(D), tile(D), tile(D)
        p_a, p_b = banks
        spread_h, among_h = (t.rearrange("p (h e) -> p h e", h=H) for t in (spread, among))

        rows_in, norm_steps, relu_ready = sem("g_rows_in"), sem("g_norm_steps"), sem("g_relu_ready")
        relu_turned, turned_sb, node_done = sem("g_relu_turned"), sem("g_turned_sb"), sem("g_node_done")
        row_ready, rows_out = sem("g_row_ready"), sem("g_rows_out")
        constants = sem("g_constants")
        a_begun, b_begun, c_begun, tiles_finished = sem("a_begun"), sem("b_begun"), sem("c_begun"), sem("tiles_finished")
        a_in, a_gathered, a_steps, feat_turned, feat_sb = sem("a_in"), sem("a_gathered"), sem("a_steps"), sem("a_feat_turned"), sem("a_feat_sb")
        a_edge_done, att_ready, spread_ready, spread_done = sem("a_edge_done"), sem("a_att_ready"), sem("a_spread_ready"), sem("a_spread_done")
        new_max_ready, max_out, att_out = sem("a_new_max_ready"), sem("a_max_out"), sem("a_att_out")
        b_in, b_gathered, b_steps, b_diff, b_exp = sem("b_in"), sem("b_gathered"), sem("b_steps"), sem("b_diff"), sem("b_exp")
        b_summed, new_sum_ready, sum_out, exp_out = sem("b_summed"), sem("b_new_sum_ready"), sem("b_sum_out"), sem("b_exp_out")
        c_in, c_gathered, c_steps, c_exp, c_message = sem("c_in"), sem("c_gathered"), sem("c_steps"), sem("c_exp"), sem("c_message")
        c_summed, new_out_ready, out_written = sem("c_summed"), sem("c_new_out_ready"), sem("c_out_written")

        block = ctx.enter_context(nc.Block())

        def applies(engine):
            return engine.If(engine.value_load(flag[0:1, 0:1], min_val=0, max_val=1) < 1)

        @block.sync
        def _(sp):
            with applies(sp):
                sp.wait_ge(constants, 3)
                with sp.Fori(0, TILES) as t:
                    here = bass.ds(t * GT, GT)
                    sp.dma_start(rows, x[here, :]).then_inc(rows_in, 16)
                    sp.dma_start(max_table[here, :], zeros[:, 0:H]).then_inc(rows_out, 16)
                    sp.dma_start(sum_table[here, :], zeros).then_inc(rows_out, 16)
                    sp.wait_ge(rows_in, t * 16 + 16)
                    sp.dma_start(out[here, :], rows).then_inc(rows_out, 16)
                    sp.wait_ge(row_ready, t + 1)
                    sp.dma_start(node_table[here, :], node_row).then_inc(rows_out, 16)
                    sp.wait_ge(rows_out, t * (4 * 16) + 4 * 16)
                    sp.sem_inc(tiles_finished, 1)

                def load_ids(t, loaded):
                    here = bass.ds(t * GT, GT)
                    sp.dma_start(src_id, src[here].unsqueeze(1)).then_inc(loaded, 16)
                    sp.dma_start(dst_id, dst[here].unsqueeze(1)).then_inc(loaded, 16)
                    sp.dma_start(dst_ids, dst[here].unsqueeze(0).broadcast_to([GT, GT])).then_inc(loaded, 16)
                    return here

                with sp.Fori(0, TILES) as t:
                    here = load_ids(t, a_in)
                    sp.dma_start(feat[:, 0:K], edge[here, :]).then_inc(a_in, 16)
                    sp.wait_ge(att_ready, t + 1)
                    sp.dma_start(edge_scratch[here, 0:H], att).then_inc(att_out, 16)
                    sp.wait_ge(max_out, t * 16 + 16)
                    sp.wait_ge(att_out, t * 16 + 16)
                    sp.sem_inc(tiles_finished, 1)

                with sp.Fori(0, TILES) as t:
                    here = load_ids(t, b_in)
                    sp.dma_start(att, edge_scratch[here, 0:H]).then_inc(b_in, 16)
                    sp.wait_ge(b_exp, t + 1)
                    sp.dma_start(edge_scratch[here, H:2 * H], ex[:, 0:H]).then_inc(exp_out, 16)
                    sp.wait_ge(sum_out, t * 16 + 16)
                    sp.wait_ge(exp_out, t * 16 + 16)
                    sp.sem_inc(tiles_finished, 1)

                with sp.Fori(0, TILES) as t:
                    here = load_ids(t, c_in)
                    sp.dma_start(ex[:, 0:H], edge_scratch[here, H:2 * H]).then_inc(c_in, 16)
                    sp.wait_ge(out_written, t * 16 + 16)
                    sp.sem_inc(tiles_finished, 1)

        @block.gpsimd
        def _(gp):
            def gather(tile, table, ids, gathered):
                gp.indirect_dma_start(out=tile, out_offset=None, in_=table,
                                      in_offset=bass.IndirectOffsetOnAxis(ap=ids, axis=0)).then_inc(gathered, 16)

            def scatter(table, tile, ids, written):
                gp.indirect_dma_start(out=table, out_offset=bass.IndirectOffsetOnAxis(ap=ids, axis=0), in_=tile,
                                      in_offset=None).then_inc(written, 16)

            with applies(gp):
                with gp.Fori(0, TILES) as t:
                    gp.wait_ge(a_in, t * (4 * 16) + 4 * 16)
                    gp.sem_inc(a_begun, 1)
                    gather(src_row, node_table, src_id, a_gathered)
                    gather(dst_row, node_table, dst_id, a_gathered)
                    gather(old_max, max_table, dst_id, a_gathered)
                    gp.wait_ge(new_max_ready, t + 1)
                    gp.sem_inc(a_begun, 1)
                    scatter(max_table, new_max, dst_id, max_out)
                with gp.Fori(0, TILES) as t:
                    gp.wait_ge(b_in, t * (4 * 16) + 4 * 16)
                    gp.sem_inc(b_begun, 1)
                    gather(dst_max, max_table, dst_id, b_gathered)
                    gather(old_sum, sum_table, dst_id, b_gathered)
                    gp.wait_ge(new_sum_ready, t + 1)
                    gp.sem_inc(b_begun, 1)
                    scatter(sum_table, new_sum, dst_id, sum_out)
                with gp.Fori(0, TILES) as t:
                    gp.wait_ge(c_in, t * (4 * 16) + 4 * 16)
                    gp.sem_inc(c_begun, 1)
                    gather(src_row, node_table, src_id, c_gathered)
                    gather(dst_max, max_table, dst_id, c_gathered)
                    gather(old_sum, sum_table, dst_id, c_gathered)
                    gather(old_out, out, dst_id, c_gathered)
                    gp.wait_ge(new_out_ready, t + 1)
                    gp.sem_inc(c_begun, 1)
                    scatter(out, new_out, dst_id, out_written)

        @block.vector
        def _(dve):
            def same_destination(t, steps, k):
                nc.vector.tensor_copy(dst_f, dst_id).then_inc(steps, 1)
                nc.vector.tensor_copy(dst_fs, dst_ids).then_inc(steps, 1)
                dve.wait_ge(steps, k(2))
                nc.vector.tensor_scalar(equal, dst_fs, dst_f, None, ALU.is_equal).then_inc(steps, 1)

            with applies(dve):
                nc.vector.memset(zeros, 0.0).then_inc(constants, 1)
                nc.vector.memset(ex[:, H:H + 1], 1.0).then_inc(constants, 1)
                nc.vector.memset(feat[:, K:2 * K], 0.0).then_inc(constants, 1)
                dve.wait_ge(constants, 3)
                with dve.Fori(0, TILES) as t:
                    k = lambda n: t * (8 + 3 * NEWTON) + n
                    dve.wait_ge(rows_in, t * 16 + 16)
                    nc.vector.tensor_reduce(total, rows, axis=AX.X, op=ALU.add).then_inc(norm_steps, 1)
                    dve.wait_ge(norm_steps, k(1))
                    nc.vector.tensor_scalar(mean, total, 1.0 / D, None, ALU.mult).then_inc(norm_steps, 1)
                    dve.wait_ge(norm_steps, k(2))
                    nc.vector.tensor_scalar(centred, rows, mean, None, ALU.subtract).then_inc(norm_steps, 1)
                    dve.wait_ge(norm_steps, k(3))
                    nc.vector.tensor_tensor(squares, centred, centred, ALU.mult).then_inc(norm_steps, 1)
                    dve.wait_ge(norm_steps, k(4))
                    nc.vector.tensor_reduce(square_sum, squares, axis=AX.X, op=ALU.add).then_inc(norm_steps, 1)
                    dve.wait_ge(norm_steps, k(5))
                    nc.vector.tensor_scalar(variance, square_sum, 1.0 / D, EPS, ALU.mult, ALU.add).then_inc(norm_steps, 1)
                    dve.wait_ge(norm_steps, k(6))
                    nc.vector.tensor_scalar(rstd.bitcast(i32), variance.bitcast(i32), -0.5, float(0x5F3759DF),
                                            ALU.mult, ALU.add).then_inc(norm_steps, 1)
                    for i in range(NEWTON):
                        dve.wait_ge(norm_steps, k(7 + 3 * i))
                        nc.vector.tensor_tensor(root, rstd, rstd, ALU.mult).then_inc(norm_steps, 1)
                        dve.wait_ge(norm_steps, k(8 + 3 * i))
                        nc.vector.scalar_tensor_tensor(root, root, -0.5, variance, ALU.mult, ALU.mult).then_inc(norm_steps, 1)
                        dve.wait_ge(norm_steps, k(9 + 3 * i))
                        nc.vector.scalar_tensor_tensor(rstd, root, 1.5, rstd, ALU.add, ALU.mult).then_inc(norm_steps, 1)
                    dve.wait_ge(norm_steps, k(7 + 3 * NEWTON))
                    nc.vector.tensor_scalar(centred, centred, rstd, None, ALU.mult).then_inc(norm_steps, 1)
                    dve.wait_ge(norm_steps, k(8 + 3 * NEWTON))
                    nc.vector.tensor_scalar(relu, centred, 0.0, None, ALU.max).then_inc(relu_ready, 1)
                    dve.wait_ge(relu_turned, t + 1)
                    nc.vector.tensor_copy(relu_T, p_a[0:D, 0:GT]).then_inc(turned_sb, 1)
                    dve.wait_ge(node_done, t + 1)
                    nc.vector.tensor_copy(node_row, p_b[0:GT, 0:HC + H]).then_inc(row_ready, 1)
                with dve.Fori(0, TILES) as t:
                    k = lambda n: t * 9 + n
                    dve.wait_ge(a_in, t * (4 * 16) + 4 * 16)
                    same_destination(t, a_steps, k)
                    dve.wait_ge(feat_turned, t + 1)
                    nc.vector.tensor_copy(feat_T, p_a[:, 0:GT]).then_inc(feat_sb, 1)
                    dve.wait_ge(a_gathered, t * (3 * 16) + 3 * 16)
                    nc.vector.tensor_tensor(z_a, src_row[:, D:HC], dst_row[:, HC:HC + H], ALU.add).then_inc(a_steps, 1)
                    dve.wait_ge(a_edge_done, t + 1)
                    dve.wait_ge(a_steps, k(4))
                    nc.vector.tensor_tensor(z_b, z_a, p_b[0:GT, 0:H], ALU.add).then_inc(a_steps, 1)
                    dve.wait_ge(a_steps, k(5))
                    nc.vector.scalar_tensor_tensor(att, z_b, 0.2, z_b, ALU.mult, ALU.max).then_inc(att_ready, 1)
                    dve.wait_ge(att_ready, t + 1)
                    nc.vector.tensor_scalar(positive, att, 0.0, None, ALU.max).then_inc(a_steps, 1)
                    dve.wait_ge(a_steps, k(6))
                    nc.vector.tensor_tensor(spread_h, ident[0:GT, 0:GT].unsqueeze(1).broadcast_to([GT, H, GT]),
                                            positive.unsqueeze(2).broadcast_to([GT, H, GT]), ALU.mult).then_inc(spread_ready, 1)
                    dve.wait_ge(spread_done, t + 1)
                    dve.wait_ge(a_steps, k(6))
                    nc.vector.tensor_tensor(among_h, p_a[0:GT, 0:H * GT].rearrange("p (h e) -> p h e", h=H),
                                            equal.unsqueeze(1).broadcast_to([GT, H, GT]), ALU.mult).then_inc(a_steps, 1)
                    dve.wait_ge(a_steps, k(7))
                    nc.vector.tensor_reduce(tile_max, among_h, axis=AX.X, op=ALU.max).then_inc(a_steps, 1)
                    dve.wait_ge(a_steps, k(8))
                    nc.vector.tensor_tensor(new_max, tile_max, old_max, ALU.max).then_inc(a_steps, 1)
                    dve.wait_ge(a_steps, k(9))
                    dve.sem_inc(new_max_ready, 1)
                with dve.Fori(0, TILES) as t:
                    k = lambda n: t * 3 + n
                    dve.wait_ge(b_in, t * (4 * 16) + 4 * 16)
                    same_destination(t, b_steps, k)
                    dve.wait_ge(b_gathered, t * (2 * 16) + 2 * 16)
                    dve.wait_ge(b_steps, k(3))
                    nc.vector.tensor_tensor(diff, att, dst_max, ALU.subtract).then_inc(b_diff, 1)
                    dve.wait_ge(b_summed, t + 1)
                    nc.vector.tensor_tensor(new_sum, old_sum, p_a[0:GT, 0:H + 1], ALU.add).then_inc(new_sum_ready, 1)
                with dve.Fori(0, TILES) as t:
                    k = lambda n: t * 8 + n
                    dve.wait_ge(c_in, t * (4 * 16) + 4 * 16)
                    same_destination(t, c_steps, k)
                    dve.wait_ge(c_gathered, t * (4 * 16) + 4 * 16)
                    nc.vector.tensor_scalar(less, old_sum[:, H:H + 1], float(E), None, ALU.subtract).then_inc(c_steps, 1)
                    dve.wait_ge(c_exp, t + 1)
                    dve.wait_ge(c_steps, k(4))
                    nc.vector.tensor_scalar(rest, em, less, None, ALU.mult).then_inc(c_steps, 1)
                    dve.wait_ge(c_steps, k(5))
                    nc.vector.tensor_tensor(den, old_sum[:, 0:H], rest, ALU.subtract).then_inc(c_steps, 1)
                    dve.wait_ge(c_steps, k(6))
                    nc.vector.reciprocal(inverse, den).then_inc(c_steps, 1)
                    dve.wait_ge(c_steps, k(7))
                    nc.vector.tensor_tensor(weight, ex[:, 0:H], inverse, ALU.mult).then_inc(c_steps, 1)
                    dve.wait_ge(c_steps, k(8))
                    nc.vector.tensor_tensor(message.rearrange("p (h j) -> p h j", h=H),
                                            src_row[:, 0:D].rearrange("p (h j) -> p h j", h=H),
                                            weight.unsqueeze(2).broadcast_to([GT, H, HD]), ALU.mult).then_inc(c_message, 1)
                    dve.wait_ge(c_summed, t + 1)
                    nc.vector.tensor_tensor(new_out, old_out, p_a[0:GT, 0:D], ALU.add).then_inc(new_out_ready, 1)

        @block.scalar
        def _(act):
            with applies(act):
                with act.Fori(0, TILES) as t:
                    act.wait_ge(b_diff, t + 1)
                    nc.scalar.activation(ex[:, 0:H], diff, ACT.Exp).then_inc(b_exp, 1)
                with act.Fori(0, TILES) as t:
                    act.wait_ge(c_gathered, t * (4 * 16) + 4 * 16)
                    nc.scalar.activation(em, dst_max, ACT.Exp, scale=-1.0).then_inc(c_exp, 1)

        @block.tensor
        def _(pe):
            with applies(pe):
                with pe.Fori(0, TILES) as t:
                    pe.wait_ge(relu_ready, t + 1)
                    nc.tensor.transpose(p_a[0:D, 0:GT], relu, ident[0:GT, 0:GT]).then_inc(relu_turned, 1)
                    pe.wait_ge(turned_sb, t + 1)
                    nc.tensor.matmul(p_b[0:GT, 0:HC], relu_T, w_h, start=True, stop=True)
                    nc.tensor.matmul(p_b[0:GT, HC:HC + H], relu_T, w_tgt, start=True, stop=True).then_inc(node_done, 1)
                with pe.Fori(0, TILES) as t:
                    pe.wait_ge(a_in, t * (4 * 16) + 4 * 16)
                    nc.tensor.transpose(p_a[:, 0:GT], feat, ident[0:GT, 0:GT]).then_inc(feat_turned, 1)
                    pe.wait_ge(feat_sb, t + 1)
                    nc.tensor.matmul(p_b[0:GT, 0:H], feat_T, w_edge, start=True, stop=True).then_inc(a_edge_done, 1)
                    pe.wait_ge(spread_ready, t + 1)
                    nc.tensor.matmul(p_a[0:GT, 0:H * GT], ones[0:GT, 0:GT], spread, start=True, stop=True).then_inc(spread_done, 1)
                with pe.Fori(0, TILES) as t:
                    pe.wait_ge(b_exp, t + 1)
                    nc.tensor.matmul(p_a[0:GT, 0:H + 1], equal, ex, start=True, stop=True).then_inc(b_summed, 1)
                with pe.Fori(0, TILES) as t:
                    pe.wait_ge(c_message, t + 1)
                    nc.tensor.matmul(p_a[0:GT, 0:D], equal, message, start=True, stop=True).then_inc(c_summed, 1)


def gat_layer(nc, x, src, dst, edge, w_node, w_edge, att, out):
    f32, i32, bf16 = mybir.dt.float32, mybir.dt.int32, mybir.dt.bfloat16
    ALU, ACT, AX = mybir.AluOpType, mybir.ActivationFunctionType, mybir.AxisListType

    N, D = x.shape
    E, K = edge.shape
    H = att.shape[0]
    HD = D // H
    EPS = 1e-5
    NEWTON = 3
    P = 128
    NT = 100
    UNITS = N // NT
    GU = 4
    STEPS = UNITS // GU
    GB = 5
    BU = GU * GB
    BATCHES = STEPS // GB
    UH = BU * H
    LONG = 4 * GB
    BR = LONG // GB
    SHORT = 4
    TURNED, TURNED_OUT, MULTIPLIED, HELD, WEIGHED, SUMMED = 0, 1, 2, 3, 3 * GB - 1, 3 * GB
    COPIED, STORED = SUMMED + 1, SUMMED + 2
    AHEAD = 3
    HC = D + H
    UC, UP = 4, UNITS // 4
    BL = 125
    NB = E // BL
    BP, BC = 100, NB // 100
    assert UNITS * NT == N and STEPS * GU == UNITS and BATCHES * GB == STEPS and NB * BL == E
    assert UC * UP == UNITS and BP * BC == NB and 2 * K == P and D == P and N == E

    start_scratch = nc.dram_tensor("window_start_scratch", (UNITS,), i32, kind="Internal").ap()
    flag_scratch = nc.dram_tensor("same_as_before_scratch", (UNITS, H, P + 1), f32, kind="Internal").ap()
    rel_scratch = nc.dram_tensor("relative_node_scratch", (UNITS * P,), bf16, kind="Internal").ap()

    ctx = ExitStack()
    with ctx:
        def sb(name, shape, dt=f32):
            return ctx.enter_context(nc.sbuf_tensor(name, shape, dt))

        def pb(name, shape, dt=f32):
            return ctx.enter_context(nc.psum_tensor(name, shape, dt))

        def sem(name):
            return ctx.enter_context(nc.semaphore(name))

        ident = sb("ident", [P, P])
        node_iota = sb("node_iota", [P, NT])
        unit_node0 = sb("unit_node0", [UP, UC])
        ones = sb("ones", [P, P])
        node_number = sb("node_number", [NT, 1])
        headmask = sb("headmask", [P, H])
        w_node_sb = sb("w_node_sb", [P, D])
        w_edge_sb = sb("w_edge_sb", [P, 2, K])
        att_col = sb("att_col", [P, 3])
        att_block = sb("att_block", [P, 3, H])
        w_h = sb("w_h", [D, HC])
        w_tgt = sb("w_tgt", [D, H])
        w_edge2 = sb("w_edge2", [P, 2, H])
        pivot = sb("pivot", [BP, BC])
        block = sb("block", [UP, UC])
        block_i = sb("block_i", [UP, UC], i32)
        inblock = sb("inblock", [UP, UC])
        first = sb("first", [UP, UC])
        first_i = sb("first_i", [UP, UC], i32)
        rel_col = sb("rel_col", [P, UNITS])
        src_col = sb("src_col", [P, UNITS], i32)
        starts = sb("starts", [1, UNITS], i32)
        idx = sb("idx", [P, BR, BU], i32)
        xs = sb("xs", [P, GB, GU, D])
        xn = sb("xn", [NT, BR, BU, D])
        hs = sb("hs", [P, BR, BU, HC])
        o = sb("o", [NT, GB, GU, D])
        mask = sb("mask", [P, SHORT, GU, NT])
        rel_row = sb("rel_row", [NT, GB, GU, P], bf16)
        maskT = sb("maskT", [NT, 2, BU, P], bf16)
        moments = sb("moments", [P, BR, BU, 2, 2, 3])
        wcol = sb("wcol", [P, BR, BU, H])
        rstd = sb("rstd", [P, BR, BU, 2])
        flags = sb("flags", [UH, BR, P + 1])
        early = hs[:, :, :, :].rearrange("p b u c -> p (b u c)")
        early_used = 0

        def early_table(shape, dt=f32):
            nonlocal early_used
            size = int(np.prod(shape[1:]))
            flat = early[0:shape[0], early_used:early_used + size].bitcast(dt)[:, 0:size]
            early_used += size
            return flat if len(shape) == 2 else flat.rearrange("p (c e) -> p c e", c=shape[1])

        dst_a = early_table([BP, BC * BL], i32)
        below = early_table([UP, NB])
        block_row = early_table([UP, UC, BL], i32)
        dst_win = early_table([UP, UC, P], i32)
        src_win = early_table([UP, UC, P], i32)
        src_winf = early_table([UP, UC, P])
        dst_rel = early_table([UP, UC, P])
        same = early_table([UP, UC, P + 1])
        rel_bf = early_table([UP, UC, P], bf16)
        order = early_table([UP, UC, P - 1])
        inside = early_table([UP, UC * P])
        inversions = sb("inversions", [UP, 1])
        from_first = sb("from_first", [UP, 1])
        past_last = sb("past_last", [UP, 1])
        held = sb("held", [UP, 1])
        all_held = sb("all_held", [1, 1])
        windows_hold = sb("windows_hold", [1, 1], i32)
        ef = sb("ef", [P, GB, GU, K])
        efT = sb("efT", [P, SHORT, 2, P])
        negmean2 = sb("negmean2", [P, SHORT, GU, 2])
        rs = sb("rs", [P, SHORT, GU, D])
        rn = sb("rn", [NT, SHORT, GU, D])
        rsT = sb("rsT", [D, SHORT, GU, P])
        rnT = sb("rnT", [D, SHORT, GU, NT])
        v = sb("v", [P, SHORT, GU, D])
        var4 = sb("var4", [P, BU, 2])
        r4 = sb("r4", [P, BU, 2])
        tgt = sb("tgt", [NT, BU, H])
        tgt_rest = sb("tgt_rest", [NT, BU, H])
        tgt_rest2 = sb("tgt_rest2", [NT, BU, H])
        tgt3 = sb("tgt3", [NT, BU, 3, H], bf16)
        z_src = sb("z_src", [P, BU, H])
        z_tgt = sb("z_tgt", [P, BU, H])
        z_a = sb("z_a", [P, BU, H])
        z_b = sb("z_b", [P, BU, H])
        z_l = sb("z_l", [P, BU, H])
        isend = sb("isend", [UH, P])
        mfwd = sb("mfwd", [UH, P])
        mend = sb("mend", [UH, P])
        mseg = sb("mseg", [UH, P])
        diff = sb("diff", [UH, P])
        ex = sb("ex", [UH, P])
        em = sb("em", [UH, P])
        cfwd = sb("cfwd", [UH, P])
        sfwd = sb("sfwd", [UH, P])
        rest = sb("rest", [UH, P])
        den = sb("den", [UH, P])
        dend = sb("dend", [UH, P])
        dseg = sb("dseg", [UH, P])
        rden = sb("rden", [UH, P])
        wrow = sb("wrow", [UH, P])

        p_src = pb("p_src", [P, GU, P])
        p_node = pb("p_node", [P, 512])
        p_z = pb("p_z", [P, 512])
        p_h = pb("p_h", [P, 2, 512])
        p_out = pb("p_out", [P, GU, D])
        p_att = pb("p_att", [P, 2, 512])
        pn = p_node[:, 0:GU * NT].rearrange("p (u n) -> p u n", u=GU)
        pe_T = p_h[:, :, 2 * HC:2 * HC + P]
        ph = p_h[:, :, 0:2 * HC].rearrange("p b (u c) -> p b u c", u=2)
        p_edge = p_att[:, :, 0:UH].rearrange("p b (u h) -> p b u h", u=BU)
        p_tgt = p_att[0:NT, :, UH:2 * UH].rearrange("p b (u h) -> p b u h", u=BU)
        p_z3 = p_att[:, :, 2 * UH:5 * UH].rearrange("p b (u k h) -> p b u k h", u=BU, k=3)
        pz_T = p_att[0:UH, :, 0:P]
        pw_c = p_z[:, 0:UH].rearrange("p (u h) -> p u h", u=BU)

        dst_loaded, w_loaded = sem("dst_loaded"), sem("w_loaded")
        const_ready, pool_const = sem("const_ready"), sem("pool_const")
        pivots_cast, pivots_spread = sem("pivots_cast"), sem("pivots_spread")
        pre, blocks_ready, blocks_loaded = sem("pre"), sem("blocks_ready"), sem("blocks_loaded")
        firsts_ready, dst_win_loaded, src_win_loaded = sem("firsts_ready"), sem("dst_win_loaded"), sem("src_win_loaded")
        starts_stored, starts_loaded = sem("starts_stored"), sem("starts_loaded")
        same_ready, same_stored = sem("same_ready"), sem("same_stored")
        relbf_ready, rel_stored = sem("relbf_ready"), sem("rel_stored")
        rel_loaded = [sem(f"rel_loaded{i}") for i in range(GB)]
        rel_ready, srcf_ready, rel_turned, src_turned = sem("rel_ready"), sem("srcf_ready"), sem("rel_turned"), sem("src_turned")
        cols_ready = sem("cols_ready")
        att_blocks, w_products, w_ready = sem("att_blocks"), sem("w_products"), sem("w_ready")
        src_gathered = [sem(f"src_gathered{i}") for i in range(GB)]
        node_loaded = [sem(f"node_loaded{i}") for i in range(LONG)]
        edge_loaded = [sem(f"edge_loaded{i}") for i in range(GB)]
        out_stored = [sem(f"out_stored{i}") for i in range(GB)]
        flags_loaded = [sem(f"flags_loaded{i}") for i in range(BR)]
        stats_raw, means_ready, mask_ready = sem("stats_raw"), sem("means_ready"), sem("mask_ready")
        src_relu, node_relu = sem("src_relu"), sem("node_relu")
        src_T, node_T, edge_T, maskT_ready = sem("src_T"), sem("node_T"), sem("edge_T"), sem("maskT_ready")
        src_T_sb, node_T_sb, edge_T_sb = sem("src_T_sb"), sem("node_T_sb"), sem("edge_T_sb")
        h_done, h_sb, tgt_done, edge_done = sem("h_done"), sem("h_sb"), sem("tgt_done"), sem("edge_done")
        v_ready, sums_done, out_ready = sem("v_ready"), sem("sums_done"), sem("out_ready")
        gathers_begun = sem("gathers_begun")
        idx_ready, var4_ready, guess_ready, rstd_steps = sem("idx_ready"), sem("var4_ready"), sem("guess_ready"), sem("rstd_steps")
        tgt_steps, tgt3_ready, z3_done = sem("tgt_steps"), sem("tgt3_ready"), sem("z3_done")
        z_steps, z_ready, z_T, flag_steps = sem("z_steps"), sem("z_ready"), sem("z_T"), sem("flag_steps")
        max_steps, mseg_ready, diff_ready = sem("max_steps"), sem("mseg_ready"), sem("diff_ready")
        em_ready, ex_ready = sem("em_ready"), sem("ex_ready")
        sum_steps, wrow_ready, w_T, w_col = sem("sum_steps"), sem("wrow_ready"), sem("w_T"), sem("w_col")

        held_steps, held_ready, held_summed, holds_ready = (sem("held_steps"), sem("held_ready"), sem("held_summed"),
                                                            sem("holds_ready"))

        windows = ExitStack()
        windows_path = windows.enter_context(nc.Block())

        def pipeline(engine, step):
            head, last = LONG + HELD + 1, STEPS + STORED + 1
            turns = (STEPS - GB - head) // LOOP
            for t in range(head):
                step(Step(None, t), t)
            with engine.Fori(0, turns) as turn:
                for t in range(head, head + LOOP):
                    step(Step(turn, t), t)
            for t in range(head + turns * LOOP, last):
                step(Step(None, t), t)

        def within(s, at_least=0):
            return s.turn is not None or at_least <= s.at < STEPS

        def wait(engine, semaphore, value):
            if not isinstance(value, int) or value > 0:
                engine.wait_ge(semaphore, value)

        def place(s):
            return (s.at // GB) % BR, slice(s.at % GB * GU, s.at % GB * GU + GU)

        @windows_path.sync
        def _(sp):
            sp.dma_start(dst_a[:, :], dst.rearrange("(p e) -> p e", p=BP)).then_inc(dst_loaded, 16)
            with nc.allow_non_contiguous_dma("the attention's vectors, once"):
                sp.dma_start(w_node_sb[:, :], w_node).then_inc(w_loaded, 16)
                for i in range(2):
                    sp.dma_start(w_edge_sb[:, i, :], w_edge).then_inc(w_loaded, 16)
                for h in range(H):
                    sp.dma_start(att_col[h * HD:(h + 1) * HD, :],
                                 att[h].rearrange("(k j) -> j k", k=3)).then_inc(w_loaded, 16)
                sp.wait_ge(firsts_ready, 1)
                sp.dma_start(start_scratch.rearrange("(c p) -> p c", c=UC), first_i[:, :]).then_inc(starts_stored, 16)
            sp.wait_ge(starts_stored, 16)
            sp.dma_start(starts[:, :], start_scratch.rearrange("(a u) -> a u", a=1)).then_inc(starts_loaded, 16)
            sp.wait_ge(relbf_ready, 1)
            sp.dma_start(rel_scratch.rearrange("(c p e) -> p c e", c=UC, p=UP), rel_bf[:, :, :]).then_inc(rel_stored, 16)
            sp.wait_ge(same_ready, 1)
            for h in range(H):
                sp.dma_start(flag_scratch[:, h, :].rearrange("(c p) e -> p c e", c=UC), same[:, :, :]).then_inc(same_stored, 16)
            sp.wait_ge(starts_loaded, 16)
            sp.wait_ge(same_stored, 16 * H)
            sp.wait_ge(rel_stored, 16)

            def load_nodes(s):
                b, us = place(s)
                wait(sp, sums_done, s.value(1, 1 - LONG))
                sp.dma_start(xn[:, b, us, :],
                             x[bass.ds(s.value(GU * NT), GU * NT), :].rearrange("(u n) d -> n u d", u=GU)
                             ).then_inc(node_loaded[s.at % LONG], 16)

            start_registers = [sp.alloc_register(f"start{u}") for u in range(GU)]

            def load_edges(s):
                wait(sp, edge_T, s.value(1, 1 - GB))
                sp.load(start_registers, starts[0:1, bass.ds(s.value(GU), GU)])
                for u in range(GU):
                    start = sp.snap(start_registers[u], min_val=0, max_val=E - P)
                    sp.dma_start(ef[:, s.at % GB, u, :], edge[bass.ds(start, P), :]).then_inc(edge_loaded[s.at % GB], 16)

            def load_rows(s):
                wait(sp, maskT_ready, s.value(1, 1 - GB))
                sp.dma_start(rel_row[:, s.at % GB, :, :].rearrange("n u e -> n (u e)"),
                             rel_scratch[bass.ds(s.value(GU * P), GU * P)].unsqueeze(0).broadcast_to([NT, GU * P])
                             ).then_inc(rel_loaded[s.at % GB], 16)

            def load_flags(s):
                wait(sp, wrow_ready, s.turns(GB, 1, 1 - BR))
                sp.dma_start(flags[:, (s.at // GB) % BR, :],
                             flag_scratch[bass.ds(s.turns(GB, BU), BU), :, :].rearrange("u h e -> (u h) e")
                             ).then_inc(flags_loaded[(s.at // GB) % BR], 16)

            def step(t, at):
                for s in ([t + n for n in range(AHEAD)] if t.turn is None and at == 0 else []) + [t + AHEAD]:
                    if within(s):
                        load_rows(s)
                        load_nodes(s)
                        load_edges(s)
                        if s.at % GB == 0:
                            load_flags(s)
                s = t + -STORED
                if within(s):
                    sp.wait_ge(out_ready, s.value(1, 1))
                    sp.dma_start(out[bass.ds(s.value(GU * NT), GU * NT), :].rearrange("(u n) d -> n u d", u=GU),
                                 o[:, s.at % GB, :, :]).then_inc(out_stored[s.at % GB], 16)

            pipeline(sp, step)
            for i in range(GB):
                sp.wait_ge(out_stored[i], 16 * len(range(i, STEPS, GB)))

        @windows_path.gpsimd
        def _(gp):
            nc.gpsimd.memset(ones[:, :], 1.0).then_inc(pool_const, 1)
            nc.gpsimd.iota(node_iota[:, :], pattern=[[1, NT]], base=0, channel_multiplier=0,
                           allow_small_or_imprecise_dtypes=True).then_inc(pool_const, 1)
            nc.gpsimd.iota(node_number[:, :], pattern=[[0, 1]], base=0, channel_multiplier=1,
                           allow_small_or_imprecise_dtypes=True).then_inc(pool_const, 1)
            nc.gpsimd.iota(unit_node0[:, :], pattern=[[NT * UP, UC]], base=0, channel_multiplier=NT,
                           allow_small_or_imprecise_dtypes=True).then_inc(pool_const, 1)
            gp.wait_ge(pool_const, 4)
            nc.gpsimd.affine_select(ident[:, :], ones[:, :], pattern=[[1, P]], compare_op=ALU.is_equal, fill=0.0,
                                    base=0, channel_multiplier=-1).then_inc(const_ready, 1)
            gp.wait_ge(blocks_ready, 1)
            for c in range(UC):
                gp.indirect_dma_start(out=block_row[:, c, :], out_offset=None, in_=dst.rearrange("(b e) -> b e", e=BL),
                                      in_offset=bass.IndirectOffsetOnAxis(ap=block_i[:, c:c + 1], axis=0)
                                      ).then_inc(blocks_loaded, 16)
            gp.wait_ge(firsts_ready, 1)
            for table, window, loaded in ((src, src_win, src_win_loaded), (dst, dst_win, dst_win_loaded)):
                for c in range(UC):
                    gp.indirect_dma_start(out=window[:, c, :], out_offset=None, in_=table.rearrange("(e a) -> e a", a=1),
                                          in_offset=bass.IndirectOffsetOnAxis(ap=first_i[:, c:c + 1], axis=0)
                                          ).then_inc(loaded, 16)

            def gather(s):
                b, us = place(s)
                wait(gp, idx_ready, s.turns(GB, 1, 1))
                wait(gp, src_relu, s.value(1, 1 - GB))
                gp.sem_inc(gathers_begun, 1)
                for i, u in enumerate(range(us.start, us.stop)):
                    gp.indirect_dma_start(out=xs[:, s.at % GB, i, :], out_offset=None, in_=x,
                                          in_offset=bass.IndirectOffsetOnAxis(ap=idx[:, b, u:u + 1], axis=0)
                                          ).then_inc(src_gathered[s.at % GB], 16)

            def step(t, at):
                if t.turn is None and at == 0:
                    for k in range(3):
                        gather(t + k)
                if within(t + 3):
                    gather(t + 3)

            pipeline(gp, step)

        @windows_path.vector
        def _(dve):
            dve.wait_ge(dst_loaded, 16)
            nc.vector.tensor_copy(pivot[:, :], dst_a[:, :].rearrange("p (c e) -> p c e", c=BC)[:, :, BL - 1]).then_inc(pivots_cast, 1)
            nc.vector.memset(moments[:, :, :, :, :, :].rearrange("p b u a c m -> p (b u a c m)"), 0.0)
            nc.vector.memset(headmask[:, :], 0.0).then_inc(pre, 1)
            dve.wait_ge(pre, 1)
            for h in range(H):
                last = nc.vector.memset(headmask[h * HD:(h + 1) * HD, h:h + 1], 1.0)
            last.then_inc(pre, 1)
            nc.vector.memset(w_edge2[:, :, :], 0.0).then_inc(pre, 1)
            dve.wait_ge(pre, 3)
            dve.wait_ge(w_loaded, 16 * (3 + H))
            for k in range(3):
                nc.vector.tensor_scalar(att_block[:, k, :], headmask[:, :], att_col[:, k:k + 1], None, ALU.mult).then_inc(att_blocks, 1)
            dve.wait_ge(pivots_spread, 1)
            dve.wait_ge(const_ready, 1)
            for c in range(UC):
                nc.vector.tensor_scalar(below[:, :], p_node[0:UP, 0:NB], unit_node0[:, c:c + 1], 0.0, ALU.is_lt, ALU.add,
                                        accum_out=block[:, c:c + 1]).then_inc(pre, 1)
                dve.wait_ge(pre, 4 + c)
            nc.vector.tensor_scalar(block[:, :], block[:, :], float(NB - 1), None, ALU.min).then_inc(pre, 1)
            dve.wait_ge(pre, 4 + UC)
            nc.vector.tensor_copy(block_i[:, :], block[:, :]).then_inc(blocks_ready, 1)
            dve.wait_ge(blocks_loaded, 16 * UC)
            for c in range(UC):
                nc.vector.tensor_scalar(below[:, 0:BL], block_row[:, c, :], unit_node0[:, c:c + 1], 0.0, ALU.is_lt, ALU.add,
                                        accum_out=inblock[:, c:c + 1]).then_inc(pre, 1)
                dve.wait_ge(pre, 5 + UC + c)
            nc.vector.scalar_tensor_tensor(first[:, :], block[:, :], float(BL), inblock[:, :], ALU.mult, ALU.add).then_inc(pre, 1)
            dve.wait_ge(pre, 5 + 2 * UC)
            nc.vector.tensor_scalar(first_i[:, :], first[:, :], float(E - P), None, ALU.min).then_inc(firsts_ready, 1)
            dve.wait_ge(src_win_loaded, 16 * UC)
            nc.vector.tensor_copy(src_winf[:, :, :], src_win[:, :, :]).then_inc(srcf_ready, 1)
            dve.wait_ge(src_turned, 1)
            nc.vector.tensor_copy(src_col[:, :], p_z[:, 0:UNITS]).then_inc(cols_ready, 1)
            dve.wait_ge(cols_ready, 1)
            for b in range(2):
                nc.vector.tensor_copy(idx[:, b, :], src_col[:, b * BU:(b + 1) * BU]).then_inc(idx_ready, 1)
            dve.wait_ge(dst_win_loaded, 16 * UC)
            nc.vector.tensor_tensor(dst_rel[:, :, :], dst_win[:, :, :],
                                    unit_node0[:, :].unsqueeze(2).broadcast_to([UP, UC, P]), ALU.subtract).then_inc(rel_ready, 1)
            dve.wait_ge(rel_ready, 1)
            nc.vector.tensor_copy(rel_bf[:, :, :], dst_rel[:, :, :]).then_inc(relbf_ready, 1)
            nc.vector.memset(same[:, :, :], 0.0).then_inc(pre, 1)
            dve.wait_ge(pre, 6 + 2 * UC)
            nc.vector.tensor_tensor(same[:, :, 1:P], dst_rel[:, :, 1:P], dst_rel[:, :, 0:P - 1], ALU.is_equal).then_inc(same_ready, 1)
            dve.wait_ge(rel_turned, 1)
            nc.vector.tensor_copy(rel_col[:, :], p_src[:, :, :].rearrange("p u e -> p (u e)")[:, 0:UNITS]).then_inc(cols_ready, 1)
            flat = dst_rel[:, :, :].rearrange("p c e -> p (c e)")
            nc.vector.tensor_scalar(inside[:, :], flat, 0.0, 0.0, ALU.is_ge, ALU.add, accum_out=from_first[:, :]).then_inc(held_steps, 1)
            nc.vector.tensor_tensor(order[:, :, :], dst_rel[:, :, 1:P], dst_rel[:, :, 0:P - 1], ALU.is_lt).then_inc(held_steps, 1)
            dve.wait_ge(held_steps, 2)
            nc.vector.tensor_scalar(inside[:, :], flat, float(NT), 0.0, ALU.is_ge, ALU.add, accum_out=past_last[:, :]).then_inc(held_steps, 1)
            nc.vector.tensor_reduce(inversions[:, :], order[:, :, :].rearrange("p c e -> p (c e)"), axis=AX.X, op=ALU.add).then_inc(held_steps, 1)
            dve.wait_ge(held_steps, 4)
            nc.vector.tensor_tensor(held[:, :], from_first[:, :], past_last[:, :], ALU.subtract).then_inc(held_steps, 1)
            dve.wait_ge(held_steps, 5)
            nc.vector.tensor_tensor(held[:, :], held[:, :], inversions[:, :], ALU.subtract).then_inc(held_ready, 1)
            dve.wait_ge(w_products, 1)
            nc.vector.tensor_copy(w_h[:, :], p_h[:, 0, 0:HC]).then_inc(w_ready, 1)
            nc.vector.tensor_copy(w_tgt[:, :], p_h[:, 1, 0:H]).then_inc(w_ready, 1)
            nc.vector.tensor_copy(w_edge2[0:K, 0, :], p_h[0:K, 1, H:2 * H]).then_inc(w_ready, 1)
            nc.vector.tensor_copy(w_edge2[K:P, 1, :], p_h[K:P, 1, H:2 * H]).then_inc(w_ready, 1)
            dve.wait_ge(cols_ready, 2)
            dve.wait_ge(held_summed, 1)
            nc.vector.tensor_copy(all_held[:, :], p_node[0:1, 0:1]).then_inc(held_steps, 1)
            dve.wait_ge(held_steps, 6)
            nc.vector.tensor_scalar(windows_hold[:, :], all_held[:, :], float(E), None, ALU.is_equal).then_inc(holds_ready, 1)

            def statistics(s, chain):
                b, us = place(s)
                dve.wait_ge(src_gathered[s.at % GB], s.turns(GB, 16 * GU, 16 * GU))
                flat = moments[:, b, :, :, :, :].rearrange("p u a c m -> p u a (c m)")
                for i, u in enumerate(range(us.start, us.stop)):
                    nc.vector.bn_stats(flat[:, u, 0, :], xs[:, s.at % GB, i, :]).then_inc(stats_raw, 1)
                    next(chain, None)
                dve.wait_ge(node_loaded[s.at % LONG], s.turns(LONG, 16, 16))
                for u in range(us.start, us.stop):
                    nc.vector.bn_stats(flat[0:NT, u, 1, :], xn[:, b, u, :]).then_inc(stats_raw, 1)
                    next(chain, None)

            def means(s):
                b, us = place(s)
                half = moments[:, b, us, :, :, :]
                wait(dve, node_relu, s.value(1, 1 - SHORT))
                dve.wait_ge(stats_raw, s.value(2 * GU, 2 * GU))
                nc.vector.scalar_tensor_tensor(negmean2[:, s.at % SHORT, :, :], half[:, :, :, 0, 1], -1.0, half[:, :, :, 1, 1],
                                               ALU.mult, ALU.subtract).then_inc(means_ready, 1)

            def masks(s):
                b, us = place(s)
                wait(dve, sums_done, s.value(1, 1 - SHORT))
                nc.vector.tensor_tensor(mask[:, s.at % SHORT, :, :], node_iota[:, :].unsqueeze(1).broadcast_to([P, GU, NT]),
                                        rel_col[:, bass.ds(s.value(GU), GU)].unsqueeze(2).broadcast_to([P, GU, NT]),
                                        ALU.is_equal).then_inc(mask_ready, 1)

            def row_masks(s):
                b, us = place(s)
                dve.wait_ge(rel_loaded[s.at % GB], s.turns(GB, 16, 16))
                wait(dve, z3_done, s.turns(GB, 1, -1))
                nc.vector.tensor_scalar(maskT[:, b % 2, us, :], rel_row[:, s.at % GB, :, :], node_number[:, 0:1], None,
                                        ALU.is_equal).then_inc(maskT_ready, 1)

            def weigh(s):
                b, us = place(s)
                dve.wait_ge(w_col, s.turns(GB, 1, 1))
                wait(dve, sums_done, s.value(1, 1 - SHORT))
                nc.vector.tensor_tensor(v[:, s.at % SHORT, :, :].rearrange("p u (h j) -> p u h j", h=H),
                                        hs[:, b, us, 0:D].rearrange("p u (h j) -> p u h j", h=H),
                                        wcol[:, b, us, :].unsqueeze(3).broadcast_to([P, GU, H, HD]),
                                        ALU.mult).then_inc(v_ready, 1)

            def batch_of(s):
                return (s.at // GB) % BR, s.turns(GB)

            def variances(s):
                b, _ = batch_of(s)
                half = moments[:, b, :, :, :, :]
                k = lambda n: s.turns(GB, 4 + 3 * NEWTON, n)
                dve.wait_ge(means_ready, s.turns(GB, GB, GB))
                nc.vector.tensor_tensor(r4[:, :, :], half[:, :, :, 0, 1], half[:, :, :, 1, 1], ALU.subtract).then_inc(rstd_steps, 1)
                nc.vector.tensor_tensor(var4[:, :, :], half[:, :, :, 0, 2], half[:, :, :, 1, 2], ALU.add).then_inc(rstd_steps, 1)
                yield
                dve.wait_ge(rstd_steps, k(2))
                nc.vector.tensor_tensor(r4[:, :, :], r4[:, :, :], r4[:, :, :], ALU.mult).then_inc(rstd_steps, 1)
                nc.vector.tensor_scalar(var4[:, :, :], var4[:, :, :], 4.0 / D, 4.0 * EPS, ALU.mult, ALU.add).then_inc(rstd_steps, 1)
                yield
                dve.wait_ge(rstd_steps, k(4))
                nc.vector.tensor_tensor(var4[:, :, :], var4[:, :, :], r4[:, :, :], ALU.add).then_inc(var4_ready, 1)
                yield
                dve.wait_ge(var4_ready, s.turns(GB, 1, 1))
                nc.vector.tensor_scalar(rstd[:, b, :, :].bitcast(i32), var4[:, :, :].bitcast(i32), -0.5, float(0x5F3759DF),
                                        ALU.mult, ALU.add).then_inc(guess_ready, 1)

            def inverse_deviations(s):
                b, _ = batch_of(s)
                r = rstd[:, b, :, :]
                k = lambda n: s.turns(GB, 4 + 3 * NEWTON, n)
                dve.wait_ge(guess_ready, s.turns(GB, 1, 1))
                for i in range(NEWTON):
                    nc.vector.tensor_tensor(r4[:, :, :], r, r, ALU.mult).then_inc(rstd_steps, 1)
                    yield
                    dve.wait_ge(rstd_steps, k(5 + 3 * i))
                    nc.vector.scalar_tensor_tensor(r4[:, :, :], r4[:, :, :], -0.5, var4[:, :, :], ALU.mult, ALU.mult).then_inc(rstd_steps, 1)
                    yield
                    dve.wait_ge(rstd_steps, k(6 + 3 * i))
                    nc.vector.scalar_tensor_tensor(r, r4[:, :, :], 1.5, r, ALU.add, ALU.mult).then_inc(rstd_steps, 1)
                    yield
                    dve.wait_ge(rstd_steps, k(7 + 3 * i))

            def targets(s):
                b, _ = batch_of(s)
                dve.wait_ge(tgt_done, s.turns(GB, GB, GB))
                wait(dve, z3_done, s.turns(GB))
                k = lambda n: s.turns(GB, 5, n)
                nc.vector.tensor_tensor(tgt[:, :, :], p_tgt[:, b % 2, :, :], rstd[0:NT, b, :, 1].unsqueeze(2).broadcast_to([NT, BU, H]),
                                        ALU.mult).then_inc(tgt_steps, 1)
                yield
                dve.wait_ge(tgt_steps, k(1))
                nc.vector.tensor_copy(tgt3[:, :, 0, :], tgt[:, :, :]).then_inc(tgt_steps, 1)
                yield
                dve.wait_ge(tgt_steps, k(2))
                nc.vector.tensor_tensor(tgt_rest[:, :, :], tgt[:, :, :], tgt3[:, :, 0, :], ALU.subtract).then_inc(tgt_steps, 1)
                yield
                dve.wait_ge(tgt_steps, k(3))
                nc.vector.tensor_copy(tgt3[:, :, 1, :], tgt_rest[:, :, :]).then_inc(tgt_steps, 1)
                yield
                dve.wait_ge(tgt_steps, k(4))
                nc.vector.tensor_tensor(tgt_rest2[:, :, :], tgt_rest[:, :, :], tgt3[:, :, 1, :], ALU.subtract).then_inc(tgt_steps, 1)
                yield
                dve.wait_ge(tgt_steps, k(5))
                nc.vector.tensor_copy(tgt3[:, :, 2, :], tgt_rest2[:, :, :]).then_inc(tgt3_ready, 1)

            def attention(s):
                b, _ = batch_of(s)
                k = lambda n: s.turns(GB, 4, n)
                dve.wait_ge(h_sb, s.turns(GB, GB, GB))
                nc.vector.tensor_tensor(z_src[:, :, :], hs[:, b, :, D:HC], rstd[:, b, :, 0].unsqueeze(2).broadcast_to([P, BU, H]),
                                        ALU.mult).then_inc(z_steps, 1)
                yield
                dve.wait_ge(edge_done, s.turns(GB, GB, GB))
                dve.wait_ge(z3_done, s.turns(GB, 1, 1))
                dve.wait_ge(z_steps, k(1))
                nc.vector.tensor_tensor(z_a[:, :, :], z_src[:, :, :], p_edge[:, b % 2, :, :], ALU.add).then_inc(z_steps, 1)
                nc.vector.tensor_reduce(z_tgt[:, :, :], p_z3[:, b % 2, :, :, :].rearrange("p u k h -> p u h k"), axis=AX.X, op=ALU.add).then_inc(z_steps, 1)
                yield
                dve.wait_ge(z_steps, k(3))
                nc.vector.tensor_tensor(z_b[:, :, :], z_a[:, :, :], z_tgt[:, :, :], ALU.add).then_inc(z_steps, 1)
                yield
                dve.wait_ge(z_steps, k(4))
                wait(dve, z_T, s.turns(GB))
                nc.vector.scalar_tensor_tensor(z_l[:, :, :], z_b[:, :, :], 0.2, z_b[:, :, :], ALU.mult, ALU.max).then_inc(z_ready, 1)

            def segments(s):
                b, _ = batch_of(s)
                dve.wait_ge(flags_loaded[b], s.turns(LONG, 16, 16))
                nc.vector.tensor_scalar(isend[:, :], flags[:, b, 1:P + 1], -1.0, 1.0, ALU.mult, ALU.add).then_inc(flag_steps, 1)
                yield
                nc.vector.tensor_tensor_scan(cfwd[:, :], flags[:, b, 0:P], ones[0:UH, :], 0.0, ALU.mult, ALU.add).then_inc(flag_steps, 1)

            def maxima(s):
                b, _ = batch_of(s)
                k = lambda n: s.turns(GB, 2, n)
                dve.wait_ge(z_T, s.turns(GB, 1, 1))
                nc.vector.tensor_tensor_scan(mfwd[:, :], flags[:, b, 0:P], pz_T[:, b % 2, :], 0.0, ALU.mult, ALU.max).then_inc(max_steps, 1)
                yield
                dve.wait_ge(max_steps, k(1))
                dve.wait_ge(flag_steps, k(1))
                nc.vector.tensor_tensor(mend[:, :], mfwd[:, :], isend[:, :], ALU.mult).then_inc(max_steps, 1)
                yield
                dve.wait_ge(max_steps, k(2))
                wait(dve, em_ready, s.turns(GB))
                nc.vector.tensor_tensor_scan(mseg[:, ::-1], flags[:, b, 1:P + 1][:, ::-1], mend[:, ::-1], 0.0,
                                             ALU.mult, ALU.max).then_inc(mseg_ready, 1)
                yield
                dve.wait_ge(mseg_ready, s.turns(GB, 1, 1))
                wait(dve, ex_ready, s.turns(GB))
                nc.vector.tensor_tensor(diff[:, :], pz_T[:, b % 2, :], mseg[:, :], ALU.subtract).then_inc(diff_ready, 1)

            def normalise(s):
                b, _ = batch_of(s)
                k = lambda n: s.turns(GB, 6, n)
                dve.wait_ge(ex_ready, s.turns(GB, 1, 1))
                nc.vector.tensor_tensor_scan(sfwd[:, :], flags[:, b, 0:P], ex[:, :], 0.0, ALU.mult, ALU.add).then_inc(sum_steps, 1)
                dve.wait_ge(em_ready, s.turns(GB, 1, 1))
                dve.wait_ge(flag_steps, s.turns(GB, 2, 2))
                nc.vector.scalar_tensor_tensor(rest[:, :], cfwd[:, :], float(E), em[:, :], ALU.subtract, ALU.mult).then_inc(sum_steps, 1)
                yield
                dve.wait_ge(sum_steps, k(2))
                nc.vector.tensor_tensor(den[:, :], sfwd[:, :], rest[:, :], ALU.subtract).then_inc(sum_steps, 1)
                yield
                dve.wait_ge(sum_steps, k(3))
                nc.vector.tensor_tensor(dend[:, :], den[:, :], isend[:, :], ALU.mult).then_inc(sum_steps, 1)
                yield
                dve.wait_ge(sum_steps, k(4))
                nc.vector.tensor_tensor_scan(dseg[:, ::-1], flags[:, b, 1:P + 1][:, ::-1], dend[:, ::-1], 0.0,
                                             ALU.mult, ALU.add).then_inc(sum_steps, 1)
                yield
                dve.wait_ge(sum_steps, k(5))
                nc.vector.reciprocal(rden[:, :], dseg[:, :]).then_inc(sum_steps, 1)
                yield
                dve.wait_ge(sum_steps, k(6))
                wait(dve, w_T, s.turns(GB))
                nc.vector.tensor_tensor(wrow[:, :], ex[:, :], rden[:, :], ALU.mult).then_inc(wrow_ready, 1)

            def weight_columns(s):
                b, _ = batch_of(s)
                dve.wait_ge(w_T, s.turns(GB, 1, 1))
                nc.vector.tensor_tensor(wcol[:, b, :, :], pw_c, rstd[:, b, :, 0].unsqueeze(2).broadcast_to([P, BU, H]),
                                        ALU.mult).then_inc(w_col, 1)
                yield

            def step(t, at):
                g = at % GB
                closing = at >= GB and within(t + -GB + -g)
                ended = at >= 2 * GB and within(t + -2 * GB + -g)
                begins, ends = [], []
                if closing:
                    if g == 0:
                        begins.append(inverse_deviations(t + -GB))
                    if g == 2:
                        ends.append(targets(t + -GB))
                    if g == 3:
                        ends.append(segments(t + -GB))
                    if g == 4:
                        ends.append(attention(t + -GB))
                if ended:
                    if g == 1:
                        begins.append(maxima(t + -2 * GB))
                    if g == 3:
                        begins.append(normalise(t + -2 * GB))
                    if g == 4:
                        ends.append(weight_columns(t + -2 * GB))
                chain = itertools.chain(*begins)
                if within(t):
                    statistics(t, chain)
                    means(t)
                    if g == 0 and at > 0 and within(t + GB):
                        nc.vector.tensor_copy(idx[:, (at // GB + 1) % BR, :],
                                              src_col[:, bass.ds(t.turns(GB, BU, BU), BU)]).then_inc(idx_ready, 1)
                    if g == GB - 1:
                        ends.append(variances(t))
                    chain = itertools.chain(chain, *ends)
                    next(chain, None)
                    row_masks(t)
                    next(chain, None)
                else:
                    chain = itertools.chain(chain, *ends)
                if within(t + -WEIGHED):
                    masks(t + -WEIGHED)
                for _ in chain:
                    pass
                if within(t + -WEIGHED):
                    weigh(t + -WEIGHED)

            pipeline(dve, step)

        @windows_path.scalar
        def _(act):
            def relu_rows(s):
                b, us = place(s)
                act.wait_ge(means_ready, s.value(1, 1))
                wait(act, src_T, s.value(1, 1 - SHORT))
                for i, u in enumerate(range(us.start, us.stop)):
                    last = nc.scalar.activation(rs[:, s.at % SHORT, i, :], xs[:, s.at % GB, i, :], ACT.Relu, scale=2.0, bias=negmean2[:, s.at % SHORT, i, 0:1])
                last.then_inc(src_relu, 1)
                wait(act, node_T, s.value(1, 1 - SHORT))
                for i, u in enumerate(range(us.start, us.stop)):
                    last = nc.scalar.activation(rn[:, s.at % SHORT, i, :], xn[:, b, u, :], ACT.Relu, scale=2.0, bias=negmean2[0:NT, s.at % SHORT, i, 1:2])
                last.then_inc(node_relu, 1)

            def step(t, at):
                g = at % GB
                if at >= 2 * GB and within(t + -2 * GB + -g) and g == 2:
                    act.wait_ge(mseg_ready, t.turns(GB, 1, -1))
                    wait(act, wrow_ready, t.turns(GB, 1, -2))
                    nc.scalar.activation(em[:, :], mseg[:, :], ACT.Exp, scale=-1.0).then_inc(em_ready, 1)
                    act.wait_ge(diff_ready, t.turns(GB, 1, -1))
                    nc.scalar.activation(ex[:, :], diff[:, :], ACT.Exp).then_inc(ex_ready, 1)
                if within(t):
                    relu_rows(t)
                s = t + -COPIED
                if within(s):
                    act.wait_ge(sums_done, s.value(1, 1))
                    wait(act, out_stored[s.at % GB], s.turns(GB, 16))
                    nc.scalar.copy(o[:, s.at % GB, :, :], p_out[0:NT, :, :]).then_inc(out_ready, 1)
                s = t + -HELD
                if within(s):
                    b, us = place(s)
                    act.wait_ge(h_done, s.value(1, 1))
                    act.wait_ge(edge_T, s.value(1, 3) if s.turn is not None else min(s.at + 3, STEPS))
                    wait(act, v_ready, s.value(1, 1 - LONG))
                    nc.scalar.copy(hs[:, b, us, :].rearrange("p (q u) c -> p q u c", q=2), ph).then_inc(h_sb, 1)
                s = t + -TURNED_OUT
                if within(s):
                    act.wait_ge(edge_T, s.value(1, 1))
                    wait(act, edge_done, s.value(1, 1 - SHORT))
                    nc.scalar.copy(efT[:, s.at % SHORT, :, :], pe_T).then_inc(edge_T_sb, 1)
                    act.wait_ge(src_T, s.value(1, 1))
                    wait(act, h_done, s.value(1, 1 - SHORT))
                    nc.scalar.copy(rsT[:, s.at % SHORT, :, :], p_src[:, :, :]).then_inc(src_T_sb, 1)
                    act.wait_ge(node_T, s.value(1, 1))
                    wait(act, tgt_done, s.value(1, 1 - SHORT))
                    nc.scalar.copy(rnT[:, s.at % SHORT, :, :], pn).then_inc(node_T_sb, 1)
            pipeline(act, step)

        @windows_path.tensor
        def _(pe):
            pe.wait_ge(const_ready, 1)
            pe.wait_ge(pivots_cast, 1)
            for c in range(BC):
                last = nc.tensor.matmul(p_node[0:UP, c * BP:(c + 1) * BP], pivot[:, c:c + 1].broadcast_to([BP, UP]),
                                        ident[0:BP, 0:BP], start=True, stop=True)
            last.then_inc(pivots_spread, 1)
            pe.wait_ge(att_blocks, 3)
            nc.tensor.transpose(p_h[:, 0, 0:D], w_node_sb[:, :], ident[:, :])
            nc.tensor.matmul(p_h[:, 0, D:HC], w_node_sb[:, :], att_block[:, 0, :], start=True, stop=True)
            nc.tensor.matmul(p_h[:, 1, 0:H], w_node_sb[:, :], att_block[:, 1, :], start=True, stop=True)
            nc.tensor.matmul(p_h[:, 1, H:2 * H], w_edge_sb[:, :, :].rearrange("p a k -> p (a k)"), att_block[:, 2, :],
                             start=True, stop=True).then_inc(w_products, 1)
            pe.wait_ge(srcf_ready, 1)
            for c in range(UC):
                last = nc.tensor.transpose(p_z[:, c * UP:(c + 1) * UP],
                                           src_winf[:, c, :], ident[0:UP, 0:UP])
            last.then_inc(src_turned, 1)
            pe.wait_ge(rel_ready, 1)
            for c in range(UC):
                last = nc.tensor.transpose(p_src[:, :, :].rearrange("p u e -> p (u e)")[:, c * UP:(c + 1) * UP],
                                           dst_rel[:, c, :], ident[0:UP, 0:UP])
            last.then_inc(rel_turned, 1)
            pe.wait_ge(held_ready, 1)
            nc.tensor.matmul(p_node[0:1, 0:1], held[:, :], ones[0:UP, 0:1], start=True, stop=True).then_inc(held_summed, 1)
            pe.wait_ge(w_ready, 4)
            pe.wait_ge(cols_ready, 2)
            pe.wait_ge(holds_ready, 1)

            def sums(s):
                b, us = place(s)
                wait(pe, out_ready, s.value())
                pe.wait_ge(node_loaded[s.at % LONG], s.turns(LONG, 16, 16))
                pe.wait_ge(v_ready, s.value(1, 1))
                for i, u in enumerate(range(us.start, us.stop)):
                    nc.tensor.matmul(p_out[0:NT, i, :], ident[0:NT, 0:NT], xn[:, b, u, :], start=True, stop=False)
                    last = nc.tensor.matmul(p_out[0:NT, i, :], mask[:, s.at % SHORT, i, :], v[:, s.at % SHORT, i, :], start=False, stop=True)
                last.then_inc(sums_done, 1)

            def bank_of_h(t):
                s = t + -MULTIPLIED
                if within(s):
                    pe.wait_ge(src_T_sb, s.value(1, 1))
                    wait(pe, h_sb, s.value())
                if within(t + -1):
                    pe.wait_ge(edge_T_sb, (t + -1).value(1, 1))
                elif t.at > 0 and within(s):
                    pe.wait_ge(edge_T_sb, STEPS)
                if within(s):
                    for i in range(GU):
                        last = nc.tensor.matmul(ph[:, i // 2, i % 2, :], rsT[:, s.at % SHORT, i, :], w_h[:, :], start=True, stop=True)
                    last.then_inc(h_done, 1)
                if within(t):
                    wait(pe, h_sb, (t + -MULTIPLIED).value())
                    pe.wait_ge(edge_loaded[t.at % GB], t.turns(GB, 16 * GU, 16 * GU))
                    for q in range(2):
                        last = nc.tensor.transpose(pe_T[:, q, :], ef[:, t.at % GB, 2 * q:2 * q + 2, :].rearrange("p u k -> p (u k)"),
                                                   ident[:, :])
                    last.then_inc(edge_T, 1)

            def products(s):
                b, us = place(s)
                pe.wait_ge(edge_T_sb, s.value(1, 1))
                wait(pe, diff_ready, s.turns(GB, 1, -1))
                for q in range(2):
                    u = us.start + 2 * q
                    last = nc.tensor.matmul(p_edge[:, b % 2, u:u + 2, :], efT[:, s.at % SHORT, q, :], w_edge2[:, :, :],
                                            start=True, stop=True)
                last.then_inc(edge_done, 1)
                pe.wait_ge(node_T_sb, s.value(1, 1))
                for i, u in enumerate(range(us.start, us.stop)):
                    last = nc.tensor.matmul(p_tgt[:, b % 2, u, :], rnT[:, s.at % SHORT, i, :], w_tgt[:, :], start=True, stop=True)
                last.then_inc(tgt_done, 1)

            def transposes(s):
                pe.wait_ge(src_relu, s.value(1, 1))
                wait(pe, src_T_sb, s.value())
                for i in range(GU):
                    last = nc.tensor.transpose(p_src[:, i, :], rs[:, s.at % SHORT, i, :], ident[:, :])
                last.then_inc(src_T, 1)
                pe.wait_ge(node_relu, s.value(1, 1))
                wait(pe, node_T_sb, s.value())
                for i in range(GU):
                    last = nc.tensor.transpose(pn[:, i, :], rn[:, s.at % SHORT, i, :], ident[0:NT, 0:NT])
                last.then_inc(node_T, 1)

            def step(t, at):
                g = at % GB
                closing = at >= GB and within(t + -GB + -g)
                ended = at >= 2 * GB and within(t + -2 * GB + -g)
                b = (at // GB - 1) % 2
                if within(t + -MULTIPLIED):
                    products(t + -MULTIPLIED)
                if closing and g == 3:
                    pe.wait_ge(tgt3_ready, t.turns(GB))
                    pe.wait_ge(maskT_ready, t.turns(GB, GB))
                    for u in range(BU):
                        last = nc.tensor.matmul(p_z3[:, b, u, :, :], maskT[:, b, u, :], tgt3[:, u, :, :], start=True, stop=True)
                    last.then_inc(z3_done, 1)
                if within(t + -SUMMED):
                    sums(t + -SUMMED)
                if ended and g == 3:
                    pe.wait_ge(wrow_ready, t.turns(GB, 1, -1))
                    wait(pe, w_col, t.turns(GB, 1, -2))
                    nc.tensor.transpose(pw_c.rearrange("p u h -> p (u h)"), wrow[:, :], ident[0:UH, 0:UH]).then_inc(w_T, 1)
                if closing and g == 4:
                    pe.wait_ge(z_ready, t.turns(GB))
                    nc.tensor.transpose(pz_T[:, b, :], z_l[:, :, :].rearrange("p u h -> p (u h)"), ident[:, :]).then_inc(z_T, 1)
                bank_of_h(t)
                if within(t + -TURNED):
                    transposes(t + -TURNED)

            pipeline(pe, step)

        windows.close()
        general_path(nc, x, src, dst, edge, out, windows_hold, w_h[:, :], w_tgt[:, :], w_edge2[:, 0, :], ident, ones,
                     hs[:, :, :, :].rearrange("p b u c -> p (b u c)"), (p_node, p_att[:, 0, :]))


_INS = ['x', 'src', 'dst', 'edge_attr_64', 'L0_gnn_W_node', 'L0_gnn_W_edge', 'L0_gnn_a']


def kernel(**inputs):
    import numpy as _np
    import concourse.bacc as _bacc
    from concourse import mybir as _mybir
    from concourse.bass_utils import run_bass_kernel_spmd as _run

    nc = _bacc.Bacc("TRN2", target_bir_lowering=False, num_devices=1)
    arrays, args = {}, []
    for name in _INS:
        a = _np.ascontiguousarray(inputs[name])
        arrays[f"in_{name}_dram"] = a
        args.append(nc.dram_tensor(f"in_{name}_dram", a.shape, _mybir.dt.from_np(a.dtype), kind="ExternalInput").ap())
    out = nc.dram_tensor("out_0_dram", arrays["in_x_dram"].shape, _mybir.dt.float32, kind="ExternalOutput").ap()
    gat_layer(nc, *args, out)
    r = _run(nc, [arrays], core_ids=[0])
    return r.results[0]["out_0_dram"]
```

```python
import numpy as np

import concourse.bass as bass
from concourse import mybir
from contextlib import ExitStack


LOOP = 20



class Step:

    def __init__(self, turn, at):
        self.turn, self.at = turn, at

    def __add__(self, n):
        return Step(self.turn, self.at + n)

    def value(self, scale=1, plus=0):
        const = scale * self.at + plus
        return const if self.turn is None else self.turn * (LOOP * scale) + const

    def turns(self, ring, scale=1, plus=0):
        const = scale * (self.at // ring) + plus
        return const if self.turn is None else self.turn * (LOOP // ring * scale) + const


def general_path(nc, x, src, dst, edge, out, flag, w_h, w_tgt, w_edge, ident, ones, ring, banks):
    f32, i32 = mybir.dt.float32, mybir.dt.int32
    ALU, ACT, AX = mybir.AluOpType, mybir.ActivationFunctionType, mybir.AxisListType

    N, D = x.shape
    E, K = edge.shape
    H = w_tgt.shape[1]
    HD = D // H
    HC = D + H
    EPS = 1e-5
    NEWTON = 3
    GT = 125
    TILES = E // GT
    assert TILES * GT == E and N == E

    node_table = nc.dram_tensor("node_table_scratch", (N, HC + H), f32, kind="Internal").ap()
    max_table = nc.dram_tensor("max_table_scratch", (N, H), f32, kind="Internal").ap()
    sum_table = nc.dram_tensor("sum_table_scratch", (N, H + 1), f32, kind="Internal").ap()
    edge_scratch = nc.dram_tensor("edge_scratch", (E, K), f32, kind="Internal").ap()

    ctx = ExitStack()
    with ctx:
        used = 0

        def tile(width):
            nonlocal used
            used += width
            return ring[0:GT, used - width:used]

        def sem(name):
            return ctx.enter_context(nc.semaphore(name))

        rows, centred, squares, relu, relu_T = tile(D), tile(D), tile(D), tile(D), ring[0:D, 4 * D:4 * D + GT]
        used += D
        total, mean, square_sum, variance, rstd, root = (tile(1) for _ in range(6))
        node_row, zeros = tile(HC + H), tile(H + 1)
        src_id, dst_id, dst_ids = tile(1).bitcast(i32), tile(1).bitcast(i32), tile(GT).bitcast(i32)
        dst_f, dst_fs, equal = tile(1), tile(GT), tile(GT)
        feat, feat_T = tile(2 * K), ring[:, used:used + GT]
        used += GT
        src_row, dst_row = tile(HC + H), tile(HC + H)
        z_a, z_b, att, positive, tile_max, old_max, new_max = (tile(H) for _ in range(7))
        spread, among = tile(H * GT), tile(H * GT)
        diff, ex, em, old_sum, new_sum = tile(H), tile(H + 1), tile(H), tile(H + 1), tile(H + 1)
        dst_max, less, rest, den, inverse, weight = tile(H), tile(1), tile(H), tile(H), tile(H), tile(H)
        message, old_out, new_out = tile(D), tile(D), tile(D)
        p_a, p_b = banks
        spread_h, among_h = (t.rearrange("p (h e) -> p h e", h=H) for t in (spread, among))

        rows_in, norm_steps, relu_ready = sem("g_rows_in"), sem("g_norm_steps"), sem("g_relu_ready")
        relu_turned, turned_sb, node_done = sem("g_relu_turned"), sem("g_turned_sb"), sem("g_node_done")
        row_ready, rows_out = sem("g_row_ready"), sem("g_rows_out")
        constants = sem("g_constants")
        a_begun, b_begun, c_begun, tiles_finished = sem("a_begun"), sem("b_begun"), sem("c_begun"), sem("tiles_finished")
        a_in, a_gathered, a_steps, feat_turned, feat_sb = sem("a_in"), sem("a_gathered"), sem("a_steps"), sem("a_feat_turned"), sem("a_feat_sb")
        a_edge_done, att_ready, spread_ready, spread_done = sem("a_edge_done"), sem("a_att_ready"), sem("a_spread_ready"), sem("a_spread_done")
        new_max_ready, max_out, att_out = sem("a_new_max_ready"), sem("a_max_out"), sem("a_att_out")
        b_in, b_gathered, b_steps, b_diff, b_exp = sem("b_in"), sem("b_gathered"), sem("b_steps"), sem("b_diff"), sem("b_exp")
        b_summed, new_sum_ready, sum_out, exp_out = sem("b_summed"), sem("b_new_sum_ready"), sem("b_sum_out"), sem("b_exp_out")
        c_in, c_gathered, c_steps, c_exp, c_message = sem("c_in"), sem("c_gathered"), sem("c_steps"), sem("c_exp"), sem("c_message")
        c_summed, new_out_ready, out_written = sem("c_summed"), sem("c_new_out_ready"), sem("c_out_written")

        block = ctx.enter_context(nc.Block())

        def applies(engine):
            return engine.If(engine.value_load(flag[0:1, 0:1], min_val=0, max_val=1) < 1)

        @block.sync
        def _(sp):
            with applies(sp):
                sp.wait_ge(constants, 3)
                with sp.Fori(0, TILES) as t:
                    here = bass.ds(t * GT, GT)
                    sp.dma_start(rows, x[here, :]).then_inc(rows_in, 16)
                    sp.dma_start(max_table[here, :], zeros[:, 0:H]).then_inc(rows_out, 16)
                    sp.dma_start(sum_table[here, :], zeros).then_inc(rows_out, 16)
                    sp.wait_ge(rows_in, t * 16 + 16)
                    sp.dma_start(out[here, :], rows).then_inc(rows_out, 16)
                    sp.wait_ge(row_ready, t + 1)
                    sp.dma_start(node_table[here, :], node_row).then_inc(rows_out, 16)
                    sp.wait_ge(rows_out, t * (4 * 16) + 4 * 16)
                    sp.sem_inc(tiles_finished, 1)

                def load_ids(t, loaded):
                    here = bass.ds(t * GT, GT)
                    sp.dma_start(src_id, src[here].unsqueeze(1)).then_inc(loaded, 16)
                    sp.dma_start(dst_id, dst[here].unsqueeze(1)).then_inc(loaded, 16)
                    sp.dma_start(dst_ids, dst[here].unsqueeze(0).broadcast_to([GT, GT])).then_inc(loaded, 16)
                    return here

                with sp.Fori(0, TILES) as t:
                    here = load_ids(t, a_in)
                    sp.dma_start(feat[:, 0:K], edge[here, :]).then_inc(a_in, 16)
                    sp.wait_ge(att_ready, t + 1)
                    sp.dma_start(edge_scratch[here, 0:H], att).then_inc(att_out, 16)
                    sp.wait_ge(max_out, t * 16 + 16)
                    sp.wait_ge(att_out, t * 16 + 16)
                    sp.sem_inc(tiles_finished, 1)

                with sp.Fori(0, TILES) as t:
                    here = load_ids(t, b_in)
                    sp.dma_start(att, edge_scratch[here, 0:H]).then_inc(b_in, 16)
                    sp.wait_ge(b_exp, t + 1)
                    sp.dma_start(edge_scratch[here, H:2 * H], ex[:, 0:H]).then_inc(exp_out, 16)
                    sp.wait_ge(sum_out, t * 16 + 16)
                    sp.wait_ge(exp_out, t * 16 + 16)
                    sp.sem_inc(tiles_finished, 1)

                with sp.Fori(0, TILES) as t:
                    here = load_ids(t, c_in)
                    sp.dma_start(ex[:, 0:H], edge_scratch[here, H:2 * H]).then_inc(c_in, 16)
                    sp.wait_ge(out_written, t * 16 + 16)
                    sp.sem_inc(tiles_finished, 1)

        @block.gpsimd
        def _(gp):
            def gather(tile, table, ids, gathered):
                gp.indirect_dma_start(out=tile, out_offset=None, in_=table,
                                      in_offset=bass.IndirectOffsetOnAxis(ap=ids, axis=0)).then_inc(gathered, 16)

            def scatter(table, tile, ids, written):
                gp.indirect_dma_start(out=table, out_offset=bass.IndirectOffsetOnAxis(ap=ids, axis=0), in_=tile,
                                      in_offset=None).then_inc(written, 16)

            with applies(gp):
                with gp.Fori(0, TILES) as t:
                    gp.wait_ge(a_in, t * (4 * 16) + 4 * 16)
                    gp.sem_inc(a_begun, 1)
                    gather(src_row, node_table, src_id, a_gathered)
                    gather(dst_row, node_table, dst_id, a_gathered)
                    gather(old_max, max_table, dst_id, a_gathered)
                    gp.wait_ge(new_max_ready, t + 1)
                    gp.sem_inc(a_begun, 1)
                    scatter(max_table, new_max, dst_id, max_out)
                with gp.Fori(0, TILES) as t:
                    gp.wait_ge(b_in, t * (4 * 16) + 4 * 16)
                    gp.sem_inc(b_begun, 1)
                    gather(dst_max, max_table, dst_id, b_gathered)
                    gather(old_sum, sum_table, dst_id, b_gathered)
                    gp.wait_ge(new_sum_ready, t + 1)
                    gp.sem_inc(b_begun, 1)
                    scatter(sum_table, new_sum, dst_id, sum_out)
                with gp.Fori(0, TILES) as t:
                    gp.wait_ge(c_in, t * (4 * 16) + 4 * 16)
                    gp.sem_inc(c_begun, 1)
                    gather(src_row, node_table, src_id, c_gathered)
                    gather(dst_max, max_table, dst_id, c_gathered)
                    gather(old_sum, sum_table, dst_id, c_gathered)
                    gather(old_out, out, dst_id, c_gathered)
                    gp.wait_ge(new_out_ready, t + 1)
                    gp.sem_inc(c_begun, 1)
                    scatter(out, new_out, dst_id, out_written)

        @block.vector
        def _(dve):
            def same_destination(t, steps, k):
                nc.vector.tensor_copy(dst_f, dst_id).then_inc(steps, 1)
                nc.vector.tensor_copy(dst_fs, dst_ids).then_inc(steps, 1)
                dve.wait_ge(steps, k(2))
                nc.vector.tensor_scalar(equal, dst_fs, dst_f, None, ALU.is_equal).then_inc(steps, 1)

            with applies(dve):
                nc.vector.memset(zeros, 0.0).then_inc(constants, 1)
                nc.vector.memset(ex[:, H:H + 1], 1.0).then_inc(constants, 1)
                nc.vector.memset(feat[:, K:2 * K], 0.0).then_inc(constants, 1)
                dve.wait_ge(constants, 3)
                with dve.Fori(0, TILES) as t:
                    k = lambda n: t * (8 + 3 * NEWTON) + n
                    dve.wait_ge(rows_in, t * 16 + 16)
                    nc.vector.tensor_reduce(total, rows, axis=AX.X, op=ALU.add).then_inc(norm_steps, 1)
                    dve.wait_ge(norm_steps, k(1))
                    nc.vector.tensor_scalar(mean, total, 1.0 / D, None, ALU.mult).then_inc(norm_steps, 1)
                    dve.wait_ge(norm_steps, k(2))
                    nc.vector.tensor_scalar(centred, rows, mean, None, ALU.subtract).then_inc(norm_steps, 1)
                    dve.wait_ge(norm_steps, k(3))
                    nc.vector.tensor_tensor(squares, centred, centred, ALU.mult).then_inc(norm_steps, 1)
                    dve.wait_ge(norm_steps, k(4))
                    nc.vector.tensor_reduce(square_sum, squares, axis=AX.X, op=ALU.add).then_inc(norm_steps, 1)
                    dve.wait_ge(norm_steps, k(5))
                    nc.vector.tensor_scalar(variance, square_sum, 1.0 / D, EPS, ALU.mult, ALU.add).then_inc(norm_steps, 1)
                    dve.wait_ge(norm_steps, k(6))
                    nc.vector.tensor_scalar(rstd.bitcast(i32), variance.bitcast(i32), -0.5, float(0x5F3759DF),
                                            ALU.mult, ALU.add).then_inc(norm_steps, 1)
                    for i in range(NEWTON):
                        dve.wait_ge(norm_steps, k(7 + 3 * i))
                        nc.vector.tensor_tensor(root, rstd, rstd, ALU.mult).then_inc(norm_steps, 1)
                        dve.wait_ge(norm_steps, k(8 + 3 * i))
                        nc.vector.scalar_tensor_tensor(root, root, -0.5, variance, ALU.mult, ALU.mult).then_inc(norm_steps, 1)
                        dve.wait_ge(norm_steps, k(9 + 3 * i))
                        nc.vector.scalar_tensor_tensor(rstd, root, 1.5, rstd, ALU.add, ALU.mult).then_inc(norm_steps, 1)
                    dve.wait_ge(norm_steps, k(7 + 3 * NEWTON))
                    nc.vector.tensor_scalar(centred, centred, rstd, None, ALU.mult).then_inc(norm_steps, 1)
                    dve.wait_ge(norm_steps, k(8 + 3 * NEWTON))
                    nc.vector.tensor_scalar(relu, centred, 0.0, None, ALU.max).then_inc(relu_ready, 1)
                    dve.wait_ge(relu_turned, t + 1)
                    nc.vector.tensor_copy(relu_T, p_a[0:D, 0:GT]).then_inc(turned_sb, 1)
                    dve.wait_ge(node_done, t + 1)
                    nc.vector.tensor_copy(node_row, p_b[0:GT, 0:HC + H]).then_inc(row_ready, 1)
                with dve.Fori(0, TILES) as t:
                    k = lambda n: t * 9 + n
                    dve.wait_ge(a_in, t * (4 * 16) + 4 * 16)
                    same_destination(t, a_steps, k)
                    dve.wait_ge(feat_turned, t + 1)
                    nc.vector.tensor_copy(feat_T, p_a[:, 0:GT]).then_inc(feat_sb, 1)
                    dve.wait_ge(a_gathered, t * (3 * 16) + 3 * 16)
                    nc.vector.tensor_tensor(z_a, src_row[:, D:HC], dst_row[:, HC:HC + H], ALU.add).then_inc(a_steps, 1)
                    dve.wait_ge(a_edge_done, t + 1)
                    dve.wait_ge(a_steps, k(4))
                    nc.vector.tensor_tensor(z_b, z_a, p_b[0:GT, 0:H], ALU.add).then_inc(a_steps, 1)
                    dve.wait_ge(a_steps, k(5))
                    nc.vector.scalar_tensor_tensor(att, z_b, 0.2, z_b, ALU.mult, ALU.max).then_inc(att_ready, 1)
                    dve.wait_ge(att_ready, t + 1)
                    nc.vector.tensor_scalar(positive, att, 0.0, None, ALU.max).then_inc(a_steps, 1)
                    dve.wait_ge(a_steps, k(6))
                    nc.vector.tensor_tensor(spread_h, ident[0:GT, 0:GT].unsqueeze(1).broadcast_to([GT, H, GT]),
                                            positive.unsqueeze(2).broadcast_to([GT, H, GT]), ALU.mult).then_inc(spread_ready, 1)
                    dve.wait_ge(spread_done, t + 1)
                    dve.wait_ge(a_steps, k(6))
                    nc.vector.tensor_tensor(among_h, p_a[0:GT, 0:H * GT].rearrange("p (h e) -> p h e", h=H),
                                            equal.unsqueeze(1).broadcast_to([GT, H, GT]), ALU.mult).then_inc(a_steps, 1)
                    dve.wait_ge(a_steps, k(7))
                    nc.vector.tensor_reduce(tile_max, among_h, axis=AX.X, op=ALU.max).then_inc(a_steps, 1)
                    dve.wait_ge(a_steps, k(8))
                    nc.vector.tensor_tensor(new_max, tile_max, old_max, ALU.max).then_inc(a_steps, 1)
                    dve.wait_ge(a_steps, k(9))
                    dve.sem_inc(new_max_ready, 1)
                with dve.Fori(0, TILES) as t:
                    k = lambda n: t * 3 + n
                    dve.wait_ge(b_in, t * (4 * 16) + 4 * 16)
                    same_destination(t, b_steps, k)
                    dve.wait_ge(b_gathered, t * (2 * 16) + 2 * 16)
                    dve.wait_ge(b_steps, k(3))
                    nc.vector.tensor_tensor(diff, att, dst_max, ALU.subtract).then_inc(b_diff, 1)
                    dve.wait_ge(b_summed, t + 1)
                    nc.vector.tensor_tensor(new_sum, old_sum, p_a[0:GT, 0:H + 1], ALU.add).then_inc(new_sum_ready, 1)
                with dve.Fori(0, TILES) as t:
                    k = lambda n: t * 8 + n
                    dve.wait_ge(c_in, t * (4 * 16) + 4 * 16)
                    same_destination(t, c_steps, k)
                    dve.wait_ge(c_gathered, t * (4 * 16) + 4 * 16)
                    nc.vector.tensor_scalar(less, old_sum[:, H:H + 1], float(E), None, ALU.subtract).then_inc(c_steps, 1)
                    dve.wait_ge(c_exp, t + 1)
                    dve.wait_ge(c_steps, k(4))
                    nc.vector.tensor_scalar(rest, em, less, None, ALU.mult).then_inc(c_steps, 1)
                    dve.wait_ge(c_steps, k(5))
                    nc.vector.tensor_tensor(den, old_sum[:, 0:H], rest, ALU.subtract).then_inc(c_steps, 1)
                    dve.wait_ge(c_steps, k(6))
                    nc.vector.reciprocal(inverse, den).then_inc(c_steps, 1)
                    dve.wait_ge(c_steps, k(7))
                    nc.vector.tensor_tensor(weight, ex[:, 0:H], inverse, ALU.mult).then_inc(c_steps, 1)
                    dve.wait_ge(c_steps, k(8))
                    nc.vector.tensor_tensor(message.rearrange("p (h j) -> p h j", h=H),
                                            src_row[:, 0:D].rearrange("p (h j) -> p h j", h=H),
                                            weight.unsqueeze(2).broadcast_to([GT, H, HD]), ALU.mult).then_inc(c_message, 1)
                    dve.wait_ge(c_summed, t + 1)
                    nc.vector.tensor_tensor(new_out, old_out, p_a[0:GT, 0:D], ALU.add).then_inc(new_out_ready, 1)

        @block.scalar
        def _(act):
            with applies(act):
                with act.Fori(0, TILES) as t:
                    act.wait_ge(b_diff, t + 1)
                    nc.scalar.activation(ex[:, 0:H], diff, ACT.Exp).then_inc(b_exp, 1)
                with act.Fori(0, TILES) as t:
                    act.wait_ge(c_gathered, t * (4 * 16) + 4 * 16)
                    nc.scalar.activation(em, dst_max, ACT.Exp, scale=-1.0).then_inc(c_exp, 1)

        @block.tensor
        def _(pe):
            with applies(pe):
                with pe.Fori(0, TILES) as t:
                    pe.wait_ge(relu_ready, t + 1)
                    nc.tensor.transpose(p_a[0:D, 0:GT], relu, ident[0:GT, 0:GT]).then_inc(relu_turned, 1)
                    pe.wait_ge(turned_sb, t + 1)
                    nc.tensor.matmul(p_b[0:GT, 0:HC], relu_T, w_h, start=True, stop=True)
                    nc.tensor.matmul(p_b[0:GT, HC:HC + H], relu_T, w_tgt, start=True, stop=True).then_inc(node_done, 1)
                with pe.Fori(0, TILES) as t:
                    pe.wait_ge(a_in, t * (4 * 16) + 4 * 16)
                    nc.tensor.transpose(p_a[:, 0:GT], feat, ident[0:GT, 0:GT]).then_inc(feat_turned, 1)
                    pe.wait_ge(feat_sb, t + 1)
                    nc.tensor.matmul(p_b[0:GT, 0:H], feat_T, w_edge, start=True, stop=True).then_inc(a_edge_done, 1)
                    pe.wait_ge(spread_ready, t + 1)
                    nc.tensor.matmul(p_a[0:GT, 0:H * GT], ones[0:GT, 0:GT], spread, start=True, stop=True).then_inc(spread_done, 1)
                with pe.Fori(0, TILES) as t:
                    pe.wait_ge(b_exp, t + 1)
                    nc.tensor.matmul(p_a[0:GT, 0:H + 1], equal, ex, start=True, stop=True).then_inc(b_summed, 1)
                with pe.Fori(0, TILES) as t:
                    pe.wait_ge(c_message, t + 1)
                    nc.tensor.matmul(p_a[0:GT, 0:D], equal, message, start=True, stop=True).then_inc(c_summed, 1)


def gat_layer(nc, x, src, dst, edge, w_node, w_edge, att, out):
    f32, i32, bf16 = mybir.dt.float32, mybir.dt.int32, mybir.dt.bfloat16
    ALU, ACT, AX = mybir.AluOpType, mybir.ActivationFunctionType, mybir.AxisListType

    N, D = x.shape
    E, K = edge.shape
    H = att.shape[0]
    HD = D // H
    EPS = 1e-5
    NEWTON = 3
    P = 128
    NT = 100
    UNITS = N // NT
    GU = 4
    STEPS = UNITS // GU
    GB = 5
    BU = GU * GB
    BATCHES = STEPS // GB
    UH = BU * H
    LONG = 4 * GB
    BR = LONG // GB
    SHORT = 4
    TURNED, TURNED_OUT, MULTIPLIED, HELD, WEIGHED, SUMMED = 0, 1, 2, 3, 3 * GB, 3 * GB + 1
    COPIED, STORED = SUMMED + 1, SUMMED + 2
    AHEAD = 3
    HC = D + H
    UC, UP = 4, UNITS // 4
    BL = 125
    NB = E // BL
    BP, BC = 100, NB // 100
    assert UNITS * NT == N and STEPS * GU == UNITS and BATCHES * GB == STEPS and NB * BL == E
    assert UC * UP == UNITS and BP * BC == NB and 2 * K == P and D == P and N == E

    start_scratch = nc.dram_tensor("window_start_scratch", (UNITS,), i32, kind="Internal").ap()
    flag_scratch = nc.dram_tensor("same_as_before_scratch", (UNITS, H, P + 1), f32, kind="Internal").ap()
    rel_scratch = nc.dram_tensor("relative_node_scratch", (UNITS * P,), bf16, kind="Internal").ap()

    ctx = ExitStack()
    with ctx:
        def sb(name, shape, dt=f32):
            return ctx.enter_context(nc.sbuf_tensor(name, shape, dt))

        def pb(name, shape, dt=f32):
            return ctx.enter_context(nc.psum_tensor(name, shape, dt))

        def sem(name):
            return ctx.enter_context(nc.semaphore(name))

        ident = sb("ident", [P, P])
        node_iota = sb("node_iota", [P, NT])
        unit_node0 = sb("unit_node0", [UP, UC])
        ones = sb("ones", [P, P])
        node_number = sb("node_number", [NT, 1])
        headmask = sb("headmask", [P, H])
        w_node_sb = sb("w_node_sb", [P, D])
        w_edge_sb = sb("w_edge_sb", [P, 2, K])
        att_col = sb("att_col", [P, 3])
        att_block = sb("att_block", [P, 3, H])
        w_h = sb("w_h", [D, HC])
        w_tgt = sb("w_tgt", [D, H])
        w_edge2 = sb("w_edge2", [P, 2, H])
        pivot = sb("pivot", [BP, BC])
        block = sb("block", [UP, UC])
        block_i = sb("block_i", [UP, UC], i32)
        inblock = sb("inblock", [UP, UC])
        first = sb("first", [UP, UC])
        first_i = sb("first_i", [UP, UC], i32)
        rel_col = sb("rel_col", [P, UNITS])
        src_col = sb("src_col", [P, UNITS], i32)
        starts = sb("starts", [1, UNITS], i32)
        idx = sb("idx", [P, BR, BU], i32)
        xs = sb("xs", [P, GB, GU, D])
        xn = sb("xn", [NT, BR, BU, D])
        hs = sb("hs", [P, BR, BU, HC])
        o = sb("o", [NT, GB, GU, D])
        mask = sb("mask", [P, SHORT, GU, NT])
        rel_row = sb("rel_row", [NT, GB, GU, P], bf16)
        maskT = sb("maskT", [NT, BR, BU, P], bf16)
        moments = sb("moments", [P, BR, BU, 2, 2, 3])
        wcol = sb("wcol", [P, BR, BU, H])
        rstd = sb("rstd", [P, BR, BU, 2])
        flags = sb("flags", [UH, BR, P + 1])
        early = hs[:, :, :, :].rearrange("p b u c -> p (b u c)")
        early_used = 0

        def early_table(shape, dt=f32):
            nonlocal early_used
            size = int(np.prod(shape[1:]))
            flat = early[0:shape[0], early_used:early_used + size].bitcast(dt)[:, 0:size]
            early_used += size
            return flat if len(shape) == 2 else flat.rearrange("p (c e) -> p c e", c=shape[1])

        dst_a = early_table([BP, BC * BL], i32)
        below = early_table([UP, NB])
        block_row = early_table([UP, UC, BL], i32)
        dst_win = early_table([UP, UC, P], i32)
        src_win = early_table([UP, UC, P], i32)
        src_winf = early_table([UP, UC, P])
        dst_rel = early_table([UP, UC, P])
        same = early_table([UP, UC, P + 1])
        rel_bf = early_table([UP, UC, P], bf16)
        order = early_table([UP, UC, P - 1])
        inside = early_table([UP, UC * P])
        inversions = sb("inversions", [UP, 1])
        from_first = sb("from_first", [UP, 1])
        past_last = sb("past_last", [UP, 1])
        held = sb("held", [UP, 1])
        all_held = sb("all_held", [1, 1])
        windows_hold = sb("windows_hold", [1, 1], i32)
        ef = sb("ef", [P, GB, GU, K])
        efT = sb("efT", [P, SHORT, 2, P])
        negmean2 = sb("negmean2", [P, SHORT, GU, 2])
        rs = sb("rs", [P, SHORT, GU, D])
        rn = sb("rn", [NT, SHORT, GU, D])
        rsT = sb("rsT", [D, SHORT, GU, P])
        rnT = sb("rnT", [D, SHORT, GU, NT])
        v = sb("v", [P, SHORT, GU, D])
        var4 = sb("var4", [P, BU, 2])
        r4 = sb("r4", [P, BU, 2])
        tgt = sb("tgt", [NT, BU, H])
        tgt_rest = sb("tgt_rest", [NT, BU, H])
        tgt3 = sb("tgt3", [NT, BU, 3, H], bf16)
        z_src = sb("z_src", [P, BU, H])
        z_tgt = sb("z_tgt", [P, BU, H])
        z_a = sb("z_a", [P, BU, H])
        z_b = z_src
        z_l = sb("z_l", [P, BU, H])
        isend = sb("isend", [UH, P])
        mfwd = sb("mfwd", [UH, P])
        mend = sb("mend", [UH, P])
        mseg = sb("mseg", [UH, P])
        diff = sb("diff", [UH, P])
        ex = sb("ex", [UH, P])
        em = sb("em", [UH, P])
        cfwd = sb("cfwd", [UH, P])
        sfwd = sb("sfwd", [UH, P])
        rest = sb("rest", [UH, P])
        den = sb("den", [UH, P])
        dend = sb("dend", [UH, P])
        dseg = sb("dseg", [UH, P])
        rden = sb("rden", [UH, P])
        wrow = sb("wrow", [UH, P])

        p_src = pb("p_src", [P, GU, P])
        p_node = pb("p_node", [P, 512])
        p_z = pb("p_z", [P, 512])
        p_h = pb("p_h", [P, 2, 512])
        p_out = pb("p_out", [P, GU, D])
        p_att = pb("p_att", [P, 2, 512])
        pn = p_node[:, 0:GU * NT].rearrange("p (u n) -> p u n", u=GU)
        pe_T = p_h[:, :, 2 * HC:2 * HC + P]
        ph = p_h[:, :, 0:2 * HC].rearrange("p b (u c) -> p b u c", u=2)
        p_edge = p_att[:, :, 0:UH].rearrange("p b (u h) -> p b u h", u=BU)
        p_tgt = p_att[0:NT, :, UH:2 * UH].rearrange("p b (u h) -> p b u h", u=BU)
        p_z3 = p_att[:, :, 2 * UH:5 * UH].rearrange("p b (u k h) -> p b u k h", u=BU, k=3)
        pz_T = p_att[0:UH, :, 0:P]
        pw_c = p_z[:, 0:UH].rearrange("p (u h) -> p u h", u=BU)

        dst_loaded, w_loaded = sem("dst_loaded"), sem("w_loaded")
        const_ready, pool_const = sem("const_ready"), sem("pool_const")
        pivots_cast, pivots_spread = sem("pivots_cast"), sem("pivots_spread")
        pre, blocks_ready, blocks_loaded = sem("pre"), sem("blocks_ready"), sem("blocks_loaded")
        firsts_ready, dst_win_loaded, src_win_loaded = sem("firsts_ready"), sem("dst_win_loaded"), sem("src_win_loaded")
        starts_stored, starts_loaded = sem("starts_stored"), sem("starts_loaded")
        same_ready, same_stored = sem("same_ready"), sem("same_stored")
        relbf_ready, rel_stored = sem("relbf_ready"), sem("rel_stored")
        rel_loaded = [sem(f"rel_loaded{i}") for i in range(GB)]
        rel_ready, srcf_ready, rel_turned, src_turned = sem("rel_ready"), sem("srcf_ready"), sem("rel_turned"), sem("src_turned")
        cols_ready = sem("cols_ready")
        att_blocks, w_products, w_ready = sem("att_blocks"), sem("w_products"), sem("w_ready")
        src_gathered = [sem(f"src_gathered{i}") for i in range(GB)]
        node_loaded = [sem(f"node_loaded{i}") for i in range(LONG)]
        edge_loaded = [sem(f"edge_loaded{i}") for i in range(GB)]
        out_stored = [sem(f"out_stored{i}") for i in range(GB)]
        flags_loaded = [sem(f"flags_loaded{i}") for i in range(BR)]
        stats_raw, means_ready = sem("stats_raw"), sem("means_ready")
        src_relu, node_relu = sem("src_relu"), sem("node_relu")
        src_T, node_T, edge_T, maskT_ready = sem("src_T"), sem("node_T"), sem("edge_T"), sem("maskT_ready")
        src_T_sb, node_T_sb, edge_T_sb = sem("src_T_sb"), sem("node_T_sb"), sem("edge_T_sb")
        h_done, h_sb, tgt_done, edge_done = sem("h_done"), sem("h_sb"), sem("tgt_done"), sem("edge_done")
        v_ready, sums_done, out_ready = sem("v_ready"), sem("sums_done"), sem("out_ready")
        gathers_begun = sem("gathers_begun")
        idx_ready, var4_ready, guess_ready, rstd_steps = sem("idx_ready"), sem("var4_ready"), sem("guess_ready"), sem("rstd_steps")
        tgt_steps, tgt3_ready, z3_done = sem("tgt_steps"), sem("tgt3_ready"), sem("z3_done")
        z_steps, z_ready, z_T, flag_steps = sem("z_steps"), sem("z_ready"), sem("z_T"), sem("flag_steps")
        max_steps, mseg_ready, diff_ready = sem("max_steps"), sem("mseg_ready"), sem("diff_ready")
        em_ready, ex_ready = sem("em_ready"), sem("ex_ready")
        sum_steps, wrow_ready, w_T, w_col = sem("sum_steps"), sem("wrow_ready"), sem("w_T"), sem("w_col")

        held_steps, held_ready = sem("held_steps"), sem("held_ready")
        held_summed, holds_ready = sem("held_summed"), sem("holds_ready")

        windows = ExitStack()
        windows_path = windows.enter_context(nc.Block())

        def pipeline(engine, step):
            head, last = LONG + HELD + 1, STEPS + STORED + 1
            turns = (STEPS - GB - head) // LOOP
            for t in range(head):
                step(Step(None, t), t)
            with engine.Fori(0, turns) as turn:
                for t in range(head, head + LOOP):
                    step(Step(turn, t), t)
            for t in range(head + turns * LOOP, last):
                step(Step(None, t), t)

        def within(s):
            return s.turn is not None or 0 <= s.at < STEPS

        def wait(engine, semaphore, value):
            if not isinstance(value, int) or value > 0:
                engine.wait_ge(semaphore, value)

        LAST_SUMS = STEPS + 2 - SUMMED

        def bank_of_sums(s):
            if s.turn is not None or s.at < LAST_SUMS:
                return p_out, 1
            if (s.at - LAST_SUMS) % 2:
                return p_src, 2
            return p_out, 1 if s.at == LAST_SUMS else 2

        def place(s):
            return (s.at // GB) % BR, slice(s.at % GB * GU, s.at % GB * GU + GU)

        @windows_path.sync
        def _(sp):
            def load_nodes(s):
                b, us = place(s)
                wait(sp, sums_done, s.value(1, 1 - LONG))
                sp.dma_start(xn[:, b, us, :],
                             x[bass.ds(s.value(GU * NT), GU * NT), :].rearrange("(u n) d -> n u d", u=GU)
                             ).then_inc(node_loaded[s.at % LONG], 16)

            start_registers = [sp.alloc_register(f"start{u}") for u in range(GU)]

            def load_edges(s):
                wait(sp, edge_T, s.value(1, 1 - GB))
                sp.load(start_registers, starts[0:1, bass.ds(s.value(GU), GU)])
                for u in range(GU):
                    start = sp.snap(start_registers[u], min_val=0, max_val=E - P)
                    sp.dma_start(ef[:, s.at % GB, u, :], edge[bass.ds(start, P), :]).then_inc(edge_loaded[s.at % GB], 16)

            def load_rows(s):
                wait(sp, maskT_ready, s.value(1, 1 - GB))
                sp.dma_start(rel_row[:, s.at % GB, :, :].rearrange("n u e -> n (u e)"),
                             rel_scratch[bass.ds(s.value(GU * P), GU * P)].unsqueeze(0).broadcast_to([NT, GU * P])
                             ).then_inc(rel_loaded[s.at % GB], 16)

            def load_flags(s):
                wait(sp, wrow_ready, s.turns(GB, 1, 1 - BR))
                sp.dma_start(flags[:, (s.at // GB) % BR, :],
                             flag_scratch[bass.ds(s.turns(GB, BU), BU), :, :].rearrange("u h e -> (u h) e")
                             ).then_inc(flags_loaded[(s.at // GB) % BR], 16)

            sp.dma_start(dst_a[:, :], dst.rearrange("(p e) -> p e", p=BP)).then_inc(dst_loaded, 16)
            with nc.allow_non_contiguous_dma("the attention's vectors, once"):
                sp.dma_start(w_node_sb[:, :], w_node).then_inc(w_loaded, 16)
                for i in range(2):
                    sp.dma_start(w_edge_sb[:, i, :], w_edge).then_inc(w_loaded, 16)
                for h in range(H):
                    sp.dma_start(att_col[h * HD:(h + 1) * HD, :],
                                 att[h].rearrange("(k j) -> j k", k=3)).then_inc(w_loaded, 16)
                sp.wait_ge(firsts_ready, 1)
                sp.dma_start(start_scratch.rearrange("(c p) -> p c", c=UC), first_i[:, :]).then_inc(starts_stored, 16)
            early_groups = [Step(None, n) for n in range(AHEAD)]
            for s in early_groups:
                load_nodes(s)
            sp.wait_ge(starts_stored, 16)
            sp.dma_start(starts[:, :], start_scratch.rearrange("(a u) -> a u", a=1)).then_inc(starts_loaded, 16)
            sp.wait_ge(starts_loaded, 16)
            for s in early_groups:
                load_edges(s)
            sp.wait_ge(relbf_ready, 1)
            sp.dma_start(rel_scratch.rearrange("(c p e) -> p c e", c=UC, p=UP), rel_bf[:, :, :]).then_inc(rel_stored, 16)
            sp.wait_ge(rel_stored, 16)
            for s in early_groups:
                load_rows(s)
            sp.wait_ge(same_ready, 1)
            for h in range(H):
                sp.dma_start(flag_scratch[:, h, :].rearrange("(c p) e -> p c e", c=UC), same[:, :, :]).then_inc(same_stored, 16)
            sp.wait_ge(same_stored, 16 * H)
            load_flags(early_groups[0])

            def step(t, at):
                s = t + AHEAD
                if within(s):
                    load_rows(s)
                    load_nodes(s)
                    load_edges(s)
                    if s.at % GB == 0:
                        load_flags(s)
                s = t + -STORED
                if within(s):
                    sp.wait_ge(out_ready, s.value(1, 1))
                    sp.dma_start(out[bass.ds(s.value(GU * NT), GU * NT), :].rearrange("(u n) d -> n u d", u=GU),
                                 o[:, s.at % GB, :, :]).then_inc(out_stored[s.at % GB], 16)

            pipeline(sp, step)
            for i in range(GB):
                sp.wait_ge(out_stored[i], 16 * len(range(i, STEPS, GB)))

        @windows_path.gpsimd
        def _(gp):
            nc.gpsimd.memset(ones[:, :], 1.0).then_inc(pool_const, 1)
            nc.gpsimd.iota(node_iota[:, :], pattern=[[1, NT]], base=0, channel_multiplier=0,
                           allow_small_or_imprecise_dtypes=True).then_inc(pool_const, 1)
            nc.gpsimd.iota(node_number[:, :], pattern=[[0, 1]], base=0, channel_multiplier=1,
                           allow_small_or_imprecise_dtypes=True).then_inc(pool_const, 1)
            nc.gpsimd.iota(unit_node0[:, :], pattern=[[NT * UP, UC]], base=0, channel_multiplier=NT,
                           allow_small_or_imprecise_dtypes=True).then_inc(pool_const, 1)
            gp.wait_ge(pool_const, 4)
            nc.gpsimd.affine_select(ident[:, :], ones[:, :], pattern=[[1, P]], compare_op=ALU.is_equal, fill=0.0,
                                    base=0, channel_multiplier=-1).then_inc(const_ready, 1)
            gp.wait_ge(blocks_ready, 1)
            for c in range(UC):
                gp.indirect_dma_start(out=block_row[:, c, :], out_offset=None, in_=dst.rearrange("(b e) -> b e", e=BL),
                                      in_offset=bass.IndirectOffsetOnAxis(ap=block_i[:, c:c + 1], axis=0)
                                      ).then_inc(blocks_loaded, 16)
            gp.wait_ge(firsts_ready, 1)
            for table, window, loaded in ((src, src_win, src_win_loaded), (dst, dst_win, dst_win_loaded)):
                for c in range(UC):
                    gp.indirect_dma_start(out=window[:, c, :], out_offset=None, in_=table.rearrange("(e a) -> e a", a=1),
                                          in_offset=bass.IndirectOffsetOnAxis(ap=first_i[:, c:c + 1], axis=0)
                                          ).then_inc(loaded, 16)

            def gather(s):
                b, us = place(s)
                wait(gp, idx_ready, s.turns(GB, 1, 1))
                wait(gp, src_relu, s.value(1, 1 - GB))
                gp.sem_inc(gathers_begun, 1)
                for i, u in enumerate(range(us.start, us.stop)):
                    gp.indirect_dma_start(out=xs[:, s.at % GB, i, :], out_offset=None, in_=x,
                                          in_offset=bass.IndirectOffsetOnAxis(ap=idx[:, b, u:u + 1], axis=0)
                                          ).then_inc(src_gathered[s.at % GB], 16)

            def step(t, at):
                if t.turn is None and at == 0:
                    for k in range(3):
                        gather(t + k)
                if within(t + 3):
                    gather(t + 3)

            pipeline(gp, step)

        @windows_path.vector
        def _(dve):
            dve.wait_ge(dst_loaded, 16)
            nc.vector.tensor_copy(pivot[:, :], dst_a[:, :].rearrange("p (c e) -> p c e", c=BC)[:, :, BL - 1]).then_inc(pivots_cast, 1)
            nc.vector.memset(moments[:, :, :, :, :, :].rearrange("p b u a c m -> p (b u a c m)"), 0.0)
            nc.vector.memset(headmask[:, :], 0.0).then_inc(pre, 1)
            dve.wait_ge(pre, 1)
            for h in range(H):
                last = nc.vector.memset(headmask[h * HD:(h + 1) * HD, h:h + 1], 1.0)
            last.then_inc(pre, 1)
            nc.vector.memset(w_edge2[:, :, :], 0.0).then_inc(pre, 1)
            dve.wait_ge(pre, 3)
            dve.wait_ge(w_loaded, 16 * (3 + H))
            for k in range(3):
                nc.vector.tensor_scalar(att_block[:, k, :], headmask[:, :], att_col[:, k:k + 1], None, ALU.mult).then_inc(att_blocks, 1)
            dve.wait_ge(pivots_spread, 1)
            dve.wait_ge(const_ready, 1)
            for c in range(UC):
                nc.vector.tensor_scalar(below[:, :], p_node[0:UP, 0:NB], unit_node0[:, c:c + 1], 0.0, ALU.is_lt, ALU.add,
                                        accum_out=block[:, c:c + 1]).then_inc(pre, 1)
                dve.wait_ge(pre, 4 + c)
            nc.vector.tensor_scalar(block[:, :], block[:, :], float(NB - 1), None, ALU.min).then_inc(pre, 1)
            dve.wait_ge(pre, 4 + UC)
            nc.vector.tensor_copy(block_i[:, :], block[:, :]).then_inc(blocks_ready, 1)
            dve.wait_ge(w_products, 1)
            nc.vector.tensor_copy(w_h[:, :], p_h[:, 0, 0:HC]).then_inc(w_ready, 1)
            nc.vector.tensor_copy(w_tgt[:, :], p_h[:, 1, 0:H]).then_inc(w_ready, 1)
            nc.vector.tensor_copy(w_edge2[0:K, 0, :], p_h[0:K, 1, H:2 * H]).then_inc(w_ready, 1)
            nc.vector.tensor_copy(w_edge2[K:P, 1, :], p_h[K:P, 1, H:2 * H]).then_inc(w_ready, 1)
            nc.vector.memset(same[:, :, :], 0.0).then_inc(pre, 1)
            dve.wait_ge(blocks_loaded, 16 * UC)
            for c in range(UC):
                nc.vector.tensor_scalar(below[:, 0:BL], block_row[:, c, :], unit_node0[:, c:c + 1], 0.0, ALU.is_lt, ALU.add,
                                        accum_out=inblock[:, c:c + 1]).then_inc(pre, 1)
                dve.wait_ge(pre, 6 + UC + c)
            nc.vector.scalar_tensor_tensor(first[:, :], block[:, :], float(BL), inblock[:, :], ALU.mult, ALU.add).then_inc(pre, 1)
            dve.wait_ge(pre, 6 + 2 * UC)
            nc.vector.tensor_scalar(first_i[:, :], first[:, :], float(E - P), None, ALU.min).then_inc(firsts_ready, 1)
            dve.wait_ge(src_win_loaded, 16 * UC)
            nc.vector.tensor_copy(src_winf[:, :, :], src_win[:, :, :]).then_inc(srcf_ready, 1)
            dve.wait_ge(src_turned, 1)
            nc.vector.tensor_copy(src_col[:, :], p_z[:, 0:UNITS]).then_inc(cols_ready, 1)
            dve.wait_ge(cols_ready, 1)
            for b in range(2):
                nc.vector.tensor_copy(idx[:, b, :], src_col[:, b * BU:(b + 1) * BU]).then_inc(idx_ready, 1)
            dve.wait_ge(dst_win_loaded, 16 * UC)
            nc.vector.tensor_tensor(dst_rel[:, :, :], dst_win[:, :, :],
                                    unit_node0[:, :].unsqueeze(2).broadcast_to([UP, UC, P]), ALU.subtract).then_inc(rel_ready, 1)
            dve.wait_ge(rel_ready, 1)
            nc.vector.tensor_copy(rel_bf[:, :, :], dst_rel[:, :, :]).then_inc(relbf_ready, 1)
            dve.wait_ge(pre, 5 + UC)
            nc.vector.tensor_tensor(same[:, :, 1:P], dst_rel[:, :, 1:P], dst_rel[:, :, 0:P - 1], ALU.is_equal).then_inc(same_ready, 1)
            dve.wait_ge(rel_turned, 1)
            nc.vector.tensor_copy(rel_col[:, :], p_src[:, :, :].rearrange("p u e -> p (u e)")[:, 0:UNITS]).then_inc(cols_ready, 1)
            dve.wait_ge(cols_ready, 2)

            def edges_held(n):
                flat = dst_rel[:, :, :].rearrange("p c e -> p (c e)")
                if n == 0:
                    nc.vector.tensor_scalar(inside[:, :], flat, 0.0, 0.0, ALU.is_ge, ALU.add, accum_out=from_first[:, :]).then_inc(held_steps, 1)
                elif n == 1:
                    nc.vector.tensor_tensor(order[:, :, :], dst_rel[:, :, 1:P], dst_rel[:, :, 0:P - 1], ALU.is_lt).then_inc(held_steps, 1)
                elif n == 2:
                    dve.wait_ge(held_steps, 2)
                    nc.vector.tensor_scalar(inside[:, :], flat, float(NT), 0.0, ALU.is_ge, ALU.add, accum_out=past_last[:, :]).then_inc(held_steps, 1)
                elif n == 3:
                    nc.vector.tensor_reduce(inversions[:, :], order[:, :, :].rearrange("p c e -> p (c e)"), axis=AX.X, op=ALU.add).then_inc(held_steps, 1)
                elif n == 4:
                    dve.wait_ge(held_steps, 4)
                    nc.vector.tensor_tensor(held[:, :], from_first[:, :], past_last[:, :], ALU.subtract).then_inc(held_steps, 1)
                elif n == 5:
                    dve.wait_ge(held_steps, 5)
                    nc.vector.tensor_tensor(held[:, :], held[:, :], inversions[:, :], ALU.subtract).then_inc(held_ready, 1)

            def windows_serve(n):
                if n == 0:
                    dve.wait_ge(held_summed, 1)
                    nc.vector.tensor_copy(all_held[:, :], p_z[0:1, 0:1]).then_inc(held_steps, 1)
                elif n == 1:
                    dve.wait_ge(held_steps, 6)
                    nc.vector.tensor_scalar(windows_hold[:, :], all_held[:, :], float(E), None, ALU.is_equal).then_inc(holds_ready, 1)

            def statistics(s, small_part):
                b, us = place(s)
                dve.wait_ge(src_gathered[s.at % GB], s.turns(GB, 16 * GU, 16 * GU))
                flat = moments[:, b, :, :, :, :].rearrange("p u a c m -> p u a (c m)")
                for i, u in enumerate(range(us.start, us.stop)):
                    nc.vector.bn_stats(flat[:, u, 0, :], xs[:, s.at % GB, i, :]).then_inc(stats_raw, 1)
                    small_part(i)
                dve.wait_ge(node_loaded[s.at % LONG], s.turns(LONG, 16, 16))
                for i, u in enumerate(range(us.start, us.stop)):
                    nc.vector.bn_stats(flat[0:NT, u, 1, :], xn[:, b, u, :]).then_inc(stats_raw, 1)
                    small_part(GU + i)

            def means(s):
                b, us = place(s)
                half = moments[:, b, us, :, :, :]
                wait(dve, node_relu, s.value(1, 1 - SHORT))
                dve.wait_ge(stats_raw, s.value(2 * GU, 2 * GU))
                nc.vector.scalar_tensor_tensor(negmean2[:, s.at % SHORT, :, :], half[:, :, :, 0, 1], -1.0, half[:, :, :, 1, 1],
                                               ALU.mult, ALU.subtract).then_inc(means_ready, 1)

            def masks(s):
                wait(dve, sums_done, s.value(1, 1 - SHORT))
                nc.vector.tensor_tensor(mask[:, s.at % SHORT, :, :], node_iota[:, :].unsqueeze(1).broadcast_to([P, GU, NT]),
                                        rel_col[:, bass.ds(s.value(GU), GU)].unsqueeze(2).broadcast_to([P, GU, NT]),
                                        ALU.is_equal)

            def row_masks(s):
                b, us = place(s)
                dve.wait_ge(rel_loaded[s.at % GB], s.turns(GB, 16, 16))
                wait(dve, z3_done, s.turns(GB, 1, 1 - BR))
                nc.vector.tensor_scalar(maskT[:, b, us, :], rel_row[:, s.at % GB, :, :], node_number[:, 0:1], None,
                                        ALU.is_equal).then_inc(maskT_ready, 1)

            def weigh(s):
                b, us = place(s)
                dve.wait_ge(w_col, s.turns(GB, 1, 1))
                wait(dve, sums_done, s.value(1, 1 - SHORT))
                nc.vector.tensor_tensor(v[:, s.at % SHORT, :, :].rearrange("p u (h j) -> p u h j", h=H),
                                        hs[:, b, us, 0:D].rearrange("p u (h j) -> p u h j", h=H),
                                        wcol[:, b, us, :].unsqueeze(3).broadcast_to([P, GU, H, HD]),
                                        ALU.mult).then_inc(v_ready, 1)

            def batch_of(s):
                return (s.at // GB) % BR, s.turns(GB)

            def variances(s, n):
                b, _ = batch_of(s)
                half = moments[:, b, :, :, :, :]
                k = lambda n: s.turns(GB, 4 + 3 * NEWTON, n)
                if n == 0:
                    dve.wait_ge(means_ready, s.turns(GB, GB, GB))
                    nc.vector.tensor_tensor(r4[:, :, :], half[:, :, :, 0, 1], half[:, :, :, 1, 1], ALU.subtract).then_inc(rstd_steps, 1)
                    nc.vector.tensor_tensor(var4[:, :, :], half[:, :, :, 0, 2], half[:, :, :, 1, 2], ALU.add).then_inc(rstd_steps, 1)
                elif n == 1:
                    dve.wait_ge(rstd_steps, k(2))
                    nc.vector.tensor_tensor(r4[:, :, :], r4[:, :, :], r4[:, :, :], ALU.mult).then_inc(rstd_steps, 1)
                    nc.vector.tensor_scalar(var4[:, :, :], var4[:, :, :], 4.0 / D, 4.0 * EPS, ALU.mult, ALU.add).then_inc(rstd_steps, 1)
                elif n == 2:
                    dve.wait_ge(rstd_steps, k(4))
                    nc.vector.tensor_tensor(var4[:, :, :], var4[:, :, :], r4[:, :, :], ALU.add).then_inc(var4_ready, 1)
                elif n == 3:
                    dve.wait_ge(var4_ready, s.turns(GB, 1, 1))
                    nc.vector.tensor_scalar(rstd[:, b, :, :].bitcast(i32), var4[:, :, :].bitcast(i32), -0.5, float(0x5F3759DF),
                                            ALU.mult, ALU.add).then_inc(guess_ready, 1)

            def inverse_deviations(s, n):
                b, _ = batch_of(s)
                r = rstd[:, b, :, :]
                if n == 0:
                    dve.wait_ge(guess_ready, s.turns(GB, 1, 1))
                elif n <= 3 * NEWTON:
                    dve.wait_ge(rstd_steps, s.turns(GB, 4 + 3 * NEWTON, 4 + n))
                if n < 3 * NEWTON and n % 3 == 0:
                    nc.vector.tensor_tensor(r4[:, :, :], r, r, ALU.mult).then_inc(rstd_steps, 1)
                elif n < 3 * NEWTON and n % 3 == 1:
                    nc.vector.scalar_tensor_tensor(r4[:, :, :], r4[:, :, :], -0.5, var4[:, :, :], ALU.mult, ALU.mult).then_inc(rstd_steps, 1)
                elif n < 3 * NEWTON:
                    nc.vector.scalar_tensor_tensor(r, r4[:, :, :], 1.5, r, ALU.add, ALU.mult).then_inc(rstd_steps, 1)

            def targets(s, n):
                b, _ = batch_of(s)
                k = lambda n: s.turns(GB, 5, n)
                if n == 0:
                    dve.wait_ge(tgt_done, s.turns(GB, GB, GB))
                    wait(dve, z3_done, s.turns(GB))
                    nc.vector.tensor_tensor(tgt[:, :, :], p_tgt[:, b % 2, :, :], rstd[0:NT, b, :, 1].unsqueeze(2).broadcast_to([NT, BU, H]),
                                            ALU.mult).then_inc(tgt_steps, 1)
                elif n == 1:
                    dve.wait_ge(tgt_steps, k(1))
                    nc.vector.tensor_copy(tgt3[:, :, 0, :], tgt[:, :, :]).then_inc(tgt_steps, 1)
                elif n == 2:
                    dve.wait_ge(tgt_steps, k(2))
                    nc.vector.tensor_tensor(tgt_rest[:, :, :], tgt[:, :, :], tgt3[:, :, 0, :], ALU.subtract).then_inc(tgt_steps, 1)
                elif n == 3:
                    dve.wait_ge(tgt_steps, k(3))
                    nc.vector.tensor_copy(tgt3[:, :, 1, :], tgt_rest[:, :, :]).then_inc(tgt_steps, 1)
                elif n == 4:
                    dve.wait_ge(tgt_steps, k(4))
                    nc.vector.tensor_tensor(tgt[:, :, :], tgt_rest[:, :, :], tgt3[:, :, 1, :], ALU.subtract).then_inc(tgt_steps, 1)
                elif n == 5:
                    dve.wait_ge(tgt_steps, k(5))
                    nc.vector.tensor_copy(tgt3[:, :, 2, :], tgt[:, :, :]).then_inc(tgt3_ready, 1)

            def attention(s, n):
                b, _ = batch_of(s)
                k = lambda n: s.turns(GB, 4, n)
                if n == 0:
                    dve.wait_ge(h_sb, s.turns(GB, GB, GB))
                    nc.vector.tensor_tensor(z_src[:, :, :], hs[:, b, :, D:HC], rstd[:, b, :, 0].unsqueeze(2).broadcast_to([P, BU, H]),
                                            ALU.mult).then_inc(z_steps, 1)
                elif n == 1:
                    dve.wait_ge(edge_done, s.turns(GB, GB, GB))
                    dve.wait_ge(z3_done, s.turns(GB, 1, 1))
                    dve.wait_ge(z_steps, k(1))
                    nc.vector.tensor_tensor(z_a[:, :, :], z_src[:, :, :], p_edge[:, b % 2, :, :], ALU.add).then_inc(z_steps, 1)
                    nc.vector.tensor_reduce(z_tgt[:, :, :], p_z3[:, b % 2, :, :, :].rearrange("p u k h -> p u h k"), axis=AX.X, op=ALU.add).then_inc(z_steps, 1)
                elif n == 2:
                    dve.wait_ge(z_steps, k(3))
                    nc.vector.tensor_tensor(z_b[:, :, :], z_a[:, :, :], z_tgt[:, :, :], ALU.add).then_inc(z_steps, 1)
                elif n == 3:
                    dve.wait_ge(z_steps, k(4))
                    wait(dve, z_T, s.turns(GB))
                    nc.vector.scalar_tensor_tensor(z_l[:, :, :], z_b[:, :, :], 0.2, z_b[:, :, :], ALU.mult, ALU.max).then_inc(z_ready, 1)

            def segments(s, n):
                b, _ = batch_of(s)
                if n == 0:
                    dve.wait_ge(flags_loaded[b], s.turns(LONG, 16, 16))
                    nc.vector.tensor_scalar(isend[:, :], flags[:, b, 1:P + 1], -1.0, 1.0, ALU.mult, ALU.add).then_inc(flag_steps, 1)
                elif n == 1:
                    nc.vector.tensor_tensor_scan(cfwd[:, :], flags[:, b, 0:P], ones[0:UH, :], 0.0, ALU.mult, ALU.add).then_inc(flag_steps, 1)

            def maxima(s, n):
                b, _ = batch_of(s)
                k = lambda n: s.turns(GB, 2, n)
                if n == 0:
                    dve.wait_ge(z_T, s.turns(GB, 1, 1))
                    nc.vector.tensor_tensor_scan(mfwd[:, :], flags[:, b, 0:P], pz_T[:, b % 2, :], 0.0, ALU.mult, ALU.max).then_inc(max_steps, 1)
                elif n == 1:
                    dve.wait_ge(max_steps, k(1))
                    dve.wait_ge(flag_steps, k(1))
                    nc.vector.tensor_tensor(mend[:, :], mfwd[:, :], isend[:, :], ALU.mult).then_inc(max_steps, 1)
                elif n == 2:
                    dve.wait_ge(max_steps, k(2))
                    wait(dve, em_ready, s.turns(GB))
                    nc.vector.tensor_tensor_scan(mseg[:, ::-1], flags[:, b, 1:P + 1][:, ::-1], mend[:, ::-1], 0.0,
                                                 ALU.mult, ALU.max).then_inc(mseg_ready, 1)
                elif n == 3:
                    dve.wait_ge(mseg_ready, s.turns(GB, 1, 1))
                    wait(dve, ex_ready, s.turns(GB))
                    nc.vector.tensor_tensor(diff[:, :], pz_T[:, b % 2, :], mseg[:, :], ALU.subtract).then_inc(diff_ready, 1)

            def normalise(s, n):
                b, _ = batch_of(s)
                k = lambda n: s.turns(GB, 6, n)
                if n == 0:
                    dve.wait_ge(ex_ready, s.turns(GB, 1, 1))
                    nc.vector.tensor_tensor_scan(sfwd[:, :], flags[:, b, 0:P], ex[:, :], 0.0, ALU.mult, ALU.add).then_inc(sum_steps, 1)
                    dve.wait_ge(em_ready, s.turns(GB, 1, 1))
                    dve.wait_ge(flag_steps, s.turns(GB, 2, 2))
                    nc.vector.scalar_tensor_tensor(rest[:, :], cfwd[:, :], float(E), em[:, :], ALU.subtract, ALU.mult).then_inc(sum_steps, 1)
                elif n == 1:
                    dve.wait_ge(sum_steps, k(2))
                    nc.vector.tensor_tensor(den[:, :], sfwd[:, :], rest[:, :], ALU.subtract).then_inc(sum_steps, 1)
                elif n == 2:
                    dve.wait_ge(sum_steps, k(3))
                    nc.vector.tensor_tensor(dend[:, :], den[:, :], isend[:, :], ALU.mult).then_inc(sum_steps, 1)
                elif n == 3:
                    dve.wait_ge(sum_steps, k(4))
                    nc.vector.tensor_tensor_scan(dseg[:, ::-1], flags[:, b, 1:P + 1][:, ::-1], dend[:, ::-1], 0.0,
                                                 ALU.mult, ALU.add).then_inc(sum_steps, 1)
                elif n == 4:
                    dve.wait_ge(sum_steps, k(5))
                    nc.vector.reciprocal(rden[:, :], dseg[:, :]).then_inc(sum_steps, 1)
                elif n == 5:
                    dve.wait_ge(sum_steps, k(6))
                    wait(dve, w_T, s.turns(GB))
                    nc.vector.tensor_tensor(wrow[:, :], ex[:, :], rden[:, :], ALU.mult).then_inc(wrow_ready, 1)

            def weight_columns(s):
                b, _ = batch_of(s)
                dve.wait_ge(w_T, s.turns(GB, 1, 1))
                nc.vector.tensor_tensor(wcol[:, b, :, :], pw_c, rstd[:, b, :, 0].unsqueeze(2).broadcast_to([P, BU, H]),
                                        ALU.mult).then_inc(w_col, 1)

            def step(t, at):
                g = at % GB
                closing = at >= GB and within(t + -GB + -g)
                ended = at >= 2 * GB and within(t + -2 * GB + -g)
                weighing = at >= 3 * GB and within(t + -3 * GB + -g)

                def small_part(n):
                    if closing and g == 0:
                        inverse_deviations(t + -GB, n)
                    if closing and g == 3:
                        targets(t + -GB, n)
                    if ended and g == 1:
                        attention(t + -2 * GB, n)
                        segments(t + -2 * GB, n - 2 * GU)
                    if ended and g == 2:
                        maxima(t + -2 * GB, n - 2 * GU)
                    if ended and g == 4:
                        normalise(t + -2 * GB, n)
                    if within(t) and g == GB - 1:
                        variances(t, n - 2 * GU)
                    if t.turn is None and at == 1:
                        edges_held(n - 2 * GU)
                    if t.turn is None and at == 3:
                        windows_serve(n - 2 * GU)

                if within(t):
                    statistics(t, small_part)
                    row_masks(t)
                    means(t)
                    if g == 0 and at > 0 and within(t + GB):
                        nc.vector.tensor_copy(idx[:, (at // GB + 1) % BR, :],
                                              src_col[:, bass.ds(t.turns(GB, BU, BU), BU)]).then_inc(idx_ready, 1)
                else:
                    for n in range(2 * GU):
                        small_part(n)
                small_part(2 * GU)
                if within(t + -WEIGHED):
                    masks(t + -WEIGHED)
                for n in range(2 * GU + 1, 2 * GU + 6):
                    small_part(n)
                if weighing and g == 0:
                    weight_columns(t + -3 * GB)
                if within(t + -WEIGHED):
                    weigh(t + -WEIGHED)

            pipeline(dve, step)

        @windows_path.scalar
        def _(act):
            def relu_rows(s):
                b, us = place(s)
                act.wait_ge(means_ready, s.value(1, 1))
                wait(act, src_T, s.value(1, 1 - SHORT))
                for i, u in enumerate(range(us.start, us.stop)):
                    last = nc.scalar.activation(rs[:, s.at % SHORT, i, :], xs[:, s.at % GB, i, :], ACT.Relu, scale=2.0, bias=negmean2[:, s.at % SHORT, i, 0:1])
                last.then_inc(src_relu, 1)
                wait(act, node_T, s.value(1, 1 - SHORT))
                for i, u in enumerate(range(us.start, us.stop)):
                    last = nc.scalar.activation(rn[:, s.at % SHORT, i, :], xn[:, b, u, :], ACT.Relu, scale=2.0, bias=negmean2[0:NT, s.at % SHORT, i, 1:2])
                last.then_inc(node_relu, 1)

            def step(t, at):
                g = at % GB
                if at >= 2 * GB and within(t + -2 * GB + -g) and g == 3:
                    act.wait_ge(mseg_ready, t.turns(GB, 1, -1))
                    wait(act, wrow_ready, t.turns(GB, 1, -2))
                    nc.scalar.activation(em[:, :], mseg[:, :], ACT.Exp, scale=-1.0).then_inc(em_ready, 1)
                    act.wait_ge(diff_ready, t.turns(GB, 1, -1))
                    nc.scalar.activation(ex[:, :], diff[:, :], ACT.Exp).then_inc(ex_ready, 1)
                if within(t):
                    relu_rows(t)
                s = t + -COPIED
                if within(s):
                    act.wait_ge(sums_done, s.value(1, 1))
                    wait(act, out_stored[s.at % GB], s.turns(GB, 16))
                    nc.scalar.copy(o[:, s.at % GB, :, :], bank_of_sums(s)[0][0:NT, :, :]).then_inc(out_ready, 1)
                s = t + -HELD
                if within(s):
                    b, us = place(s)
                    act.wait_ge(h_done, s.value(1, 1))
                    act.wait_ge(edge_T, s.value(1, 3) if s.turn is not None else min(s.at + 3, STEPS))
                    wait(act, v_ready, s.value(1, 1 - LONG))
                    nc.scalar.copy(hs[:, b, us, :].rearrange("p (q u) c -> p q u c", q=2), ph).then_inc(h_sb, 1)
                s = t + -TURNED_OUT
                if within(s):
                    act.wait_ge(edge_T, s.value(1, 1))
                    wait(act, edge_done, s.value(1, 1 - SHORT))
                    nc.scalar.copy(efT[:, s.at % SHORT, :, :], pe_T).then_inc(edge_T_sb, 1)
                    act.wait_ge(src_T, s.value(1, 1))
                    wait(act, h_done, s.value(1, 1 - SHORT))
                    nc.scalar.copy(rsT[:, s.at % SHORT, :, :], p_src[:, :, :]).then_inc(src_T_sb, 1)
                    act.wait_ge(node_T, s.value(1, 1))
                    wait(act, tgt_done, s.value(1, 1 - SHORT))
                    nc.scalar.copy(rnT[:, s.at % SHORT, :, :], pn).then_inc(node_T_sb, 1)
            pipeline(act, step)

        @windows_path.tensor
        def _(pe):
            pe.wait_ge(const_ready, 1)
            pe.wait_ge(pivots_cast, 1)
            for c in range(BC):
                last = nc.tensor.matmul(p_node[0:UP, c * BP:(c + 1) * BP], pivot[:, c:c + 1].broadcast_to([BP, UP]),
                                        ident[0:BP, 0:BP], start=True, stop=True)
            last.then_inc(pivots_spread, 1)
            pe.wait_ge(att_blocks, 3)
            nc.tensor.transpose(p_h[:, 0, 0:D], w_node_sb[:, :], ident[:, :])
            nc.tensor.matmul(p_h[:, 0, D:HC], w_node_sb[:, :], att_block[:, 0, :], start=True, stop=True)
            nc.tensor.matmul(p_h[:, 1, 0:H], w_node_sb[:, :], att_block[:, 1, :], start=True, stop=True)
            nc.tensor.matmul(p_h[:, 1, H:2 * H], w_edge_sb[:, :, :].rearrange("p a k -> p (a k)"), att_block[:, 2, :],
                             start=True, stop=True).then_inc(w_products, 1)
            pe.wait_ge(srcf_ready, 1)
            for c in range(UC):
                last = nc.tensor.transpose(p_z[:, c * UP:(c + 1) * UP],
                                           src_winf[:, c, :], ident[0:UP, 0:UP])
            last.then_inc(src_turned, 1)
            pe.wait_ge(rel_ready, 1)
            for c in range(UC):
                last = nc.tensor.transpose(p_src[:, :, :].rearrange("p u e -> p (u e)")[:, c * UP:(c + 1) * UP],
                                           dst_rel[:, c, :], ident[0:UP, 0:UP])
            last.then_inc(rel_turned, 1)
            pe.wait_ge(w_ready, 4)
            pe.wait_ge(cols_ready, 2)

            def sums(s):
                b, us = place(s)
                sums_bank, before = bank_of_sums(s)
                wait(pe, out_ready, s.value(1, 1 - before))
                if s.turn is None and s.at == LAST_SUMS:
                    pe.wait_ge(src_T_sb, STEPS)
                pe.wait_ge(node_loaded[s.at % LONG], s.turns(LONG, 16, 16))
                nc.tensor.matmul(sums_bank[0:NT, :, :], ident[0:NT, 0:NT], xn[:, b, us, :], start=True, stop=False)
                pe.wait_ge(v_ready, s.value(1, 1))
                for i in range(GU):
                    last = nc.tensor.matmul(sums_bank[0:NT, i, :], mask[:, s.at % SHORT, i, :], v[:, s.at % SHORT, i, :],
                                            start=False, stop=i == GU - 1)
                last.then_inc(sums_done, 1)

            def bank_of_h(t):
                s = t + -MULTIPLIED
                if within(s):
                    pe.wait_ge(src_T_sb, s.value(1, 1))
                    wait(pe, h_sb, s.value())
                if within(t + -1):
                    pe.wait_ge(edge_T_sb, (t + -1).value(1, 1))
                elif t.at > 0 and within(s):
                    pe.wait_ge(edge_T_sb, STEPS)
                if within(s):
                    for i in range(GU):
                        last = nc.tensor.matmul(ph[:, i // 2, i % 2, :], rsT[:, s.at % SHORT, i, :], w_h[:, :], start=True, stop=True)
                    last.then_inc(h_done, 1)
                if within(t):
                    wait(pe, h_sb, (t + -MULTIPLIED).value())
                    pe.wait_ge(edge_loaded[t.at % GB], t.turns(GB, 16 * GU, 16 * GU))
                    for q in range(2):
                        last = nc.tensor.transpose(pe_T[:, q, :], ef[:, t.at % GB, 2 * q:2 * q + 2, :].rearrange("p u k -> p (u k)"),
                                                   ident[:, :])
                    last.then_inc(edge_T, 1)

            def products(s):
                b, us = place(s)
                pe.wait_ge(edge_T_sb, s.value(1, 1))
                wait(pe, diff_ready, s.turns(GB, 1, -1))
                for q in range(2):
                    u = us.start + 2 * q
                    last = nc.tensor.matmul(p_edge[:, b % 2, u:u + 2, :], efT[:, s.at % SHORT, q, :], w_edge2[:, :, :],
                                            start=True, stop=True)
                last.then_inc(edge_done, 1)
                pe.wait_ge(node_T_sb, s.value(1, 1))
                for i, u in enumerate(range(us.start, us.stop)):
                    last = nc.tensor.matmul(p_tgt[:, b % 2, u, :], rnT[:, s.at % SHORT, i, :], w_tgt[:, :], start=True, stop=True)
                last.then_inc(tgt_done, 1)

            def transposes(s):
                pe.wait_ge(src_relu, s.value(1, 1))
                wait(pe, src_T_sb, s.value())
                for i in range(GU):
                    last = nc.tensor.transpose(p_src[:, i, :], rs[:, s.at % SHORT, i, :], ident[:, :])
                last.then_inc(src_T, 1)
                pe.wait_ge(node_relu, s.value(1, 1))
                wait(pe, node_T_sb, s.value())
                for i in range(GU):
                    last = nc.tensor.transpose(pn[:, i, :], rn[:, s.at % SHORT, i, :], ident[0:NT, 0:NT])
                last.then_inc(node_T, 1)

            def step(t, at):
                g = at % GB
                closing = at >= GB and within(t + -GB + -g)
                ended = at >= 2 * GB and within(t + -2 * GB + -g)
                b = (at // GB - 1) % 2
                if t.turn is None and at == MULTIPLIED:
                    pe.wait_ge(held_ready, 1)
                    nc.tensor.matmul(p_z[0:1, 0:1], held[:, :], ones[0:UP, 0:1], start=True, stop=True).then_inc(held_summed, 1)
                    pe.wait_ge(rel_stored, 16)
                    pe.wait_ge(same_stored, 16 * H)
                if ended and g == 1:
                    pe.wait_ge(z_ready, t.turns(GB, 1, -1))
                    nc.tensor.transpose(pz_T[:, 1 - b, :], z_l[:, :, :].rearrange("p u h -> p (u h)"), ident[:, :]).then_inc(z_T, 1)
                if ended and g == 4:
                    pe.wait_ge(wrow_ready, t.turns(GB, 1, -1))
                    if t.turn is None:
                        pe.wait_ge(holds_ready, 1)
                    wait(pe, w_col, t.turns(GB, 1, -2))
                    nc.tensor.transpose(pw_c.rearrange("p u h -> p (u h)"), wrow[:, :], ident[0:UH, 0:UH]).then_inc(w_T, 1)
                if within(t + -MULTIPLIED):
                    products(t + -MULTIPLIED)
                if closing and g == 4:
                    pe.wait_ge(tgt3_ready, t.turns(GB))
                    pe.wait_ge(maskT_ready, t.turns(GB, GB))
                    for u in range(BU):
                        last = nc.tensor.matmul(p_z3[:, b, u, :, :], maskT[:, (at // GB - 1) % BR, u, :], tgt3[:, u, :, :], start=True, stop=True)
                    last.then_inc(z3_done, 1)
                if within(t + -SUMMED):
                    sums(t + -SUMMED)
                bank_of_h(t)
                if within(t + -TURNED):
                    transposes(t + -TURNED)

            pipeline(pe, step)

        windows.close()
        general_path(nc, x, src, dst, edge, out, windows_hold, w_h[:, :], w_tgt[:, :], w_edge2[:, 0, :], ident, ones,
                     hs[:, :, :, :].rearrange("p b u c -> p (b u c)"), (p_node, p_att[:, 0, :]))


_INS = ['x', 'src', 'dst', 'edge_attr_64', 'L0_gnn_W_node', 'L0_gnn_W_edge', 'L0_gnn_a']


def kernel(**inputs):
    import numpy as _np
    import concourse.bacc as _bacc
    from concourse import mybir as _mybir
    from concourse.bass_utils import run_bass_kernel_spmd as _run

    nc = _bacc.Bacc("TRN2", target_bir_lowering=False, num_devices=1)
    arrays, args = {}, []
    for name in _INS:
        a = _np.ascontiguousarray(inputs[name])
        arrays[f"in_{name}_dram"] = a
        args.append(nc.dram_tensor(f"in_{name}_dram", a.shape, _mybir.dt.from_np(a.dtype), kind="ExternalInput").ap())
    out = nc.dram_tensor("out_0_dram", arrays["in_x_dram"].shape, _mybir.dt.float32, kind="ExternalOutput").ap()
    gat_layer(nc, *args, out)
    r = _run(nc, [arrays], core_ids=[0])
    return r.results[0]["out_0_dram"]
```
